# Optimizing a Trainium2 kernel written in Bass

```python
import numpy as np
import jax
import jax.numpy as jnp

def _softmax(x, axis=-1):
    return jax.nn.softmax(x, axis=axis)

def _gelu(x):
    return jax.nn.gelu(x, approximate=True)

def _silu(x):
    return jax.nn.silu(x)

def _sigmoid(x):
    return jax.nn.sigmoid(x)

def _layernorm(x, axis=-1, eps=1e-05):
    m = jnp.mean(x, axis=axis, keepdims=True)
    v = jnp.var(x, axis=axis, keepdims=True)
    return (x - m) / jnp.sqrt(v + eps)

def _scatter_add(tgt, idx, src, axis=0):
    return tgt.at[idx].add(src)

def _segment_sum(src, seg, n):
    return jax.ops.segment_sum(src, seg, n)
kernel_name = 'mk_adj_preln_d2_adj_r2_253ead'

def setup_inputs(seed: int=0):
    np.random.seed(seed)
    _w = jnp.asarray

    def _rec_inputs():
        import jax
        import jax.numpy as jnp
        _gk = jax.random.key(seed)
        x = -0.0002928 + 1 * jax.random.normal(jax.random.fold_in(_gk, 1), (64, 128, 128), jnp.float32)
        _a = jax.random.bernoulli(jax.random.fold_in(_gk, 2), 0.125, (64, 128, 128))
        _a = jnp.logical_or(_a, jnp.swapaxes(_a, -1, -2))
        _a = jnp.logical_or(_a, jnp.eye(128, dtype=bool))
        _af = _a.astype(jnp.float32)
        _af = _af * jax.random.uniform(jax.random.fold_in(_gk, 3), (64, 128, 128), jnp.float32, 0.05, 1)
        adj = _af
        return (x, adj)
    x, adj = _rec_inputs()

    def _L0_gnn_setup():
        import jax, jax.numpy as jnp
        import numpy as np
        B, N, D, H = (8, 1024, 128, 512)
        RMS_EPS = 1e-06

        def _rmsnorm(h, w, eps=RMS_EPS):
            var = jnp.mean(jnp.square(h), axis=-1, keepdims=True)
            return h * jax.lax.rsqrt(var + eps) * w
        key = jax.random.key(seed)
        ks = jax.random.split(key, 5)
        x = jax.random.normal(ks[0], (B, N, D), dtype=jnp.float32)
        adjacency = jax.random.uniform(ks[1], (B, N, N), dtype=jnp.float32)
        epsilon = jnp.zeros((), dtype=jnp.float32)
        W1 = jax.random.normal(ks[2], (D, H), dtype=jnp.float32) * (1.0 / np.sqrt(D))
        b1 = jnp.zeros((H,), dtype=jnp.float32)
        rms_weight = jnp.ones((H,), dtype=jnp.float32)
        W2 = jax.random.normal(ks[3], (H, D), dtype=jnp.float32) * (1.0 / np.sqrt(H))
        b2 = jnp.zeros((D,), dtype=jnp.float32)
        return {'x': x, 'adjacency': adjacency, 'epsilon': epsilon, 'W1': W1, 'b1': b1, 'rms_weight': rms_weight, 'W2': W2, 'b2': b2}
    _L0_gnn_all = _L0_gnn_setup()
    _L0_gnn_in = {k: v for k, v in _L0_gnn_all.items() if k in ('epsilon', 'W1', 'b1', 'rms_weight', 'W2', 'b2')}
    del _L0_gnn_all

    def _L1_gnn_setup():
        import jax, jax.numpy as jnp
        import numpy as np
        from jax import lax
        DIM = 128
        EPS = 1e-05

        def _bn(h, g, b, m, v):
            scale = g / jnp.sqrt(v + EPS)
            return h * scale[None, :, None] + (b - m * scale)[None, :, None]

        def _conv1d(h, w, pad):
            return lax.conv_general_dilated(h, w, window_strides=(1,), padding=[(pad, pad)], dimension_numbers=('NCH', 'OIH', 'NCH'))
        key = jax.random.key(seed)
        ks = jax.random.split(key, 16)
        bs, n, d = (16, 1024, DIM)
        s = 0.05
        return {'x': jax.random.normal(ks[0], (bs, n, d), jnp.float32), 'mask': jnp.ones((bs, n, n), jnp.float32), 'w_se': jax.random.normal(ks[1], (3, d), jnp.float32) * s, 'b_se': jnp.zeros((3,), jnp.float32), 'conv1_w': jax.random.normal(ks[2], (d, d, 1), jnp.float32) * s, 'bn1_g': jnp.ones((d,), jnp.float32), 'bn1_b': jnp.zeros((d,), jnp.float32), 'bn1_m': jnp.zeros((d,), jnp.float32), 'bn1_v': jnp.ones((d,), jnp.float32), 'conv2_w': jax.random.normal(ks[3], (d, d, 17), jnp.float32) * s, 'bn2_g': jnp.ones((d,), jnp.float32), 'bn2_b': jnp.zeros((d,), jnp.float32), 'bn2_m': jnp.zeros((d,), jnp.float32), 'bn2_v': jnp.ones((d,), jnp.float32), 'w_msg': jax.random.normal(ks[4], (d, d), jnp.float32) * s, 'b_msg': jnp.zeros((d,), jnp.float32), 'w_ih': jax.random.normal(ks[5], (3 * d, 2 * d), jnp.float32) * s, 'b_ih': jnp.zeros((3 * d,), jnp.float32), 'w_hh': jax.random.normal(ks[6], (3 * d, d), jnp.float32) * s, 'b_hh': jnp.zeros((3 * d,), jnp.float32)}
    _L1_gnn_all = _L1_gnn_setup()
    _L1_gnn_in = {k: v for k, v in _L1_gnn_all.items() if k in ('w_se', 'b_se', 'conv1_w', 'bn1_g', 'bn1_b', 'bn1_m', 'bn1_v', 'conv2_w', 'bn2_g', 'bn2_b', 'bn2_m', 'bn2_v', 'w_msg', 'b_msg', 'w_ih', 'b_ih', 'w_hh', 'b_hh')}
    del _L1_gnn_all
    return {'x': x, 'adj': adj, 'L0_gnn_epsilon': _L0_gnn_in['epsilon'], 'L0_gnn_W1': _L0_gnn_in['W1'], 'L0_gnn_b1': _L0_gnn_in['b1'], 'L0_gnn_rms_weight': _L0_gnn_in['rms_weight'], 'L0_gnn_W2': _L0_gnn_in['W2'], 'L0_gnn_b2': _L0_gnn_in['b2'], 'L1_gnn_w_se': _L1_gnn_in['w_se'], 'L1_gnn_b_se': _L1_gnn_in['b_se'], 'L1_gnn_conv1_w': _L1_gnn_in['conv1_w'], 'L1_gnn_bn1_g': _L1_gnn_in['bn1_g'], 'L1_gnn_bn1_b': _L1_gnn_in['bn1_b'], 'L1_gnn_bn1_m': _L1_gnn_in['bn1_m'], 'L1_gnn_bn1_v': _L1_gnn_in['bn1_v'], 'L1_gnn_conv2_w': _L1_gnn_in['conv2_w'], 'L1_gnn_bn2_g': _L1_gnn_in['bn2_g'], 'L1_gnn_bn2_b': _L1_gnn_in['bn2_b'], 'L1_gnn_bn2_m': _L1_gnn_in['bn2_m'], 'L1_gnn_bn2_v': _L1_gnn_in['bn2_v'], 'L1_gnn_w_msg': _L1_gnn_in['w_msg'], 'L1_gnn_b_msg': _L1_gnn_in['b_msg'], 'L1_gnn_w_ih': _L1_gnn_in['w_ih'], 'L1_gnn_b_ih': _L1_gnn_in['b_ih'], 'L1_gnn_w_hh': _L1_gnn_in['w_hh'], 'L1_gnn_b_hh': _L1_gnn_in['b_hh']}

def reference(x, adj, L0_gnn_epsilon, L0_gnn_W1, L0_gnn_b1, L0_gnn_rms_weight, L0_gnn_W2, L0_gnn_b2, L1_gnn_w_se, L1_gnn_b_se, L1_gnn_conv1_w, L1_gnn_bn1_g, L1_gnn_bn1_b, L1_gnn_bn1_m, L1_gnn_bn1_v, L1_gnn_conv2_w, L1_gnn_bn2_g, L1_gnn_bn2_b, L1_gnn_bn2_m, L1_gnn_bn2_v, L1_gnn_w_msg, L1_gnn_b_msg, L1_gnn_w_ih, L1_gnn_b_ih, L1_gnn_w_hh, L1_gnn_b_hh):
    import jax
    import jax.numpy as jnp

    def _L0_gnn_ref(x, adjacency, epsilon, W1, b1, rms_weight, W2, b2):
        import jax, jax.numpy as jnp
        import numpy as np
        B, N, D, H = (8, 1024, 128, 512)
        RMS_EPS = 1e-06

        def _rmsnorm(h, w, eps=RMS_EPS):
            var = jnp.mean(jnp.square(h), axis=-1, keepdims=True)
            return h * jax.lax.rsqrt(var + eps) * w
        neighbor_sum = jnp.einsum('bnm,bmd->bnd', adjacency, x)
        agg = epsilon * x + neighbor_sum
        h = jnp.einsum('bnd,dh->bnh', agg, W1) + b1
        h = jax.nn.silu(_rmsnorm(h, rms_weight))
        out = jnp.einsum('bnh,hd->bnd', h, W2) + b2
        return out

    def _L1_gnn_ref(x, mask, w_se, b_se, conv1_w, bn1_g, bn1_b, bn1_m, bn1_v, conv2_w, bn2_g, bn2_b, bn2_m, bn2_v, w_msg, b_msg, w_ih, b_ih, w_hh, b_hh):
        import jax, jax.numpy as jnp
        import numpy as np
        from jax import lax
        DIM = 128
        EPS = 1e-05

        def _bn(h, g, b, m, v):
            scale = g / jnp.sqrt(v + EPS)
            return h * scale[None, :, None] + (b - m * scale)[None, :, None]

        def _conv1d(h, w, pad):
            return lax.conv_general_dilated(h, w, window_strides=(1,), padding=[(pad, pad)], dimension_numbers=('NCH', 'OIH', 'NCH'))
        d = x.shape[-1]
        xc = jnp.transpose(x, (0, 2, 1))
        h = _bn(_conv1d(xc, conv1_w, 0), bn1_g, bn1_b, bn1_m, bn1_v)
        h = jax.nn.relu(h)
        h = _bn(_conv1d(h, conv2_w, 8), bn2_g, bn2_b, bn2_m, bn2_v)
        x_conv = jnp.transpose(jax.nn.relu(h + xc), (0, 2, 1))
        s = x @ w_se.T + b_se
        sq = jnp.sum(s * s, axis=-1)
        dist = sq[:, :, None] + sq[:, None, :] - 2.0 * jnp.einsum('bnd,bmd->bnm', s, s)
        A = jnp.exp(-dist) * mask
        msg = jax.nn.relu(x @ w_msg.T + b_msg)
        x_nmp = jnp.einsum('bnm,bmd->bnd', A, msg)
        x_in = jnp.concatenate([x_conv, x_nmp], axis=-1)
        gi = x_in @ w_ih.T + b_ih
        gh = x @ w_hh.T + b_hh
        gi_r, gi_z, gi_n = (gi[..., :d], gi[..., d:2 * d], gi[..., 2 * d:])
        gh_r, gh_z, gh_n = (gh[..., :d], gh[..., d:2 * d], gh[..., 2 * d:])
        r = jax.nn.sigmoid(gi_r + gh_r)
        z = jax.nn.sigmoid(gi_z + gh_z)
        nn_ = jnp.tanh(gi_n + r * gh_n)
        return (1.0 - z) * nn_ + z * x
    h = jnp.maximum(_layernorm(x, axis=-1), 0.0)
    x = x + _L0_gnn_ref(h, adj, L0_gnn_epsilon, L0_gnn_W1, L0_gnn_b1, L0_gnn_rms_weight, L0_gnn_W2, L0_gnn_b2)
    h = jnp.maximum(_layernorm(x, axis=-1), 0.0)
    x = x + _L1_gnn_ref(h, adj, L1_gnn_w_se, L1_gnn_b_se, L1_gnn_conv1_w, L1_gnn_bn1_g, L1_gnn_bn1_b, L1_gnn_bn1_m, L1_gnn_bn1_v, L1_gnn_conv2_w, L1_gnn_bn2_g, L1_gnn_bn2_b, L1_gnn_bn2_m, L1_gnn_bn2_v, L1_gnn_w_msg, L1_gnn_b_msg, L1_gnn_w_ih, L1_gnn_b_ih, L1_gnn_w_hh, L1_gnn_b_hh)
    return x

_drawn_inputs = setup_inputs


def setup_inputs(seed=0):
    import zlib

    import numpy as np

    out = dict(_drawn_inputs(seed))
    spreads = {'L0_gnn_b1': (0.0, 0.797),
     'L0_gnn_rms_weight': (1.0, 0.2),
     'L0_gnn_b2': (0.0, 0.1),
     'L1_gnn_b_se': (0.0, 0.8),
     'L1_gnn_bn1_g': (1.0, 0.6),
     'L1_gnn_bn1_b': (0.0, 0.462),
     'L1_gnn_bn1_m': (0.0, 0.434),
     'L1_gnn_bn1_v': (1.0, 0.6),
     'L1_gnn_bn2_g': (1.0, 0.6),
     'L1_gnn_bn2_b': (0.0, 0.704),
     'L1_gnn_bn2_m': (0.0, 0.625),
     'L1_gnn_bn2_v': (1.0, 0.6),
     'L1_gnn_b_msg': (0.0, 0.1),
     'L1_gnn_b_ih': (0.0, 0.338),
     'L1_gnn_b_hh': (0.0, 0.483)}
    factors = {}
    for name, (base, spread) in spreads.items():
        noise = np.random.default_rng([zlib.crc32(name.encode()), seed]).standard_normal(out[name].shape)
        drawn = base * np.exp(spread * noise) if base else spread * noise
        out[name] = jnp.asarray(drawn.astype(out[name].dtype))
    for name, factor in factors.items():
        out[name] = (out[name] * factor).astype(out[name].dtype)
    return out
```

```python
from contextlib import ExitStack

import numpy as np

import concourse.bass as bass
from concourse import mybir
from concourse.alu_op_type import AluOpType as ALU

F32 = mybir.dt.float32
F32R = mybir.dt.float32r
ACT = mybir.ActivationFunctionType

P = 128
GRAPHS = 64
PER = 4
T = PER * P
NG = GRAPHS // PER
HC = 4
TAPS = 17
HALF = TAPS // 2
PADDED = P + 2
LN_EPS, RMS_EPS, BN_EPS = 1e-5, 1e-6, 1e-5
SEEDS = 3
LOOP_FIRST, LOOP_END = 2, 12

W_COLS = {"w1": HC * P, "conv1": P, "msg": P, "hh": 3 * P, "w2": HC * P, "ih": 6 * P, "conv2": TAPS * P}
W_AT = {}
for _name in W_COLS:
    W_AT[_name] = sum(W_COLS[n] for n in W_AT)
W_TOTAL = sum(W_COLS.values())

V_NAMES = (["b1_0", "b1_1", "b1_2", "b1_3", "rms_0", "rms_1", "rms_2", "rms_3", "b2", "bse",
            "bn1_g", "bn2_g", "bn1_b", "bn2_b", "bn1_m", "bn2_m", "bn1_v", "bn2_v",
            "bih_r", "bih_z", "bih_n", "bhh_r", "bhh_z", "bhh_n"])
V_AT = {n: i for i, n in enumerate(V_NAMES)}


def build(nc, x_nodes, x_feats, adj_t, weights, w_se, vectors, b_msg, epsilon, out):
    with ExitStack() as ctx:
        def sb(name, shape, dt=F32):
            return ctx.enter_context(nc.sbuf_tensor(name, shape, dt))

        def sem(name):
            return ctx.enter_context(nc.semaphore(name))

        w_hi = sb("w_hi", [P, W_TOTAL], F32R)
        w_lo = sb("w_lo", [P, W_TOTAL], F32R)
        RAW = T * 4 + P
        w_raw = sb("w_raw", [P, RAW])
        w_se_sb = sb("w_se_sb", [P, P])
        vec = sb("vec", [P, len(V_NAMES)])
        b_msg_sb = sb("b_msg_sb", [P, PER, P])
        eps_col = sb("eps_col", [P, 1])
        eye = sb("eye", [P, P])
        eps_eye = sb("eps_eye", [P, PER, P])
        ones = sb("ones", [P, P])
        mean_col = sb("mean_col", [P, 1])
        minus_half = sb("minus_half", [P, PER])
        hb_bias = sb("hb_bias", [P, HC])
        bn_scale = sb("bn_scale", [P, 2])
        bn_root = sb("bn_root", [P, 2])
        bn_inv = sb("bn_inv", [P, 2])
        bn_ms = sb("bn_ms", [P, 2])
        bn_bias = sb("bn_bias", [P, 2])
        gate_sum = sb("gate_sum", [P, 2])
        gate_bias = sb("gate_bias", [P, 2])

        x_in = sb("x_in", [P, 2, PER, P])
        adj_in = sb("adj_in", [P, 2, PER, P])
        xT_in = sb("xT_in", [P, 2, T])
        mask_in = sb("mask_in", [P, 2, PER, P])
        stats1 = sb("stats1", [P, PER, 6])
        moments1 = sb("moments1", [P, PER, 2])
        var1 = sb("var1", [P, PER])
        rstd1 = sb("rstd1", [P, PER])
        shift1 = sb("shift1", [P, PER])
        norm1 = sb("norm1", [P, PER, P])
        h1 = sb("h1", [P, PER, P])
        adj_eps = sb("adj_eps", [P, PER, P])
        agg_hi = sb("agg_hi", [P, T], F32R)
        agg_lo = sb("agg_lo", [P, T], F32R)
        sq = sb("sq", [P, HC, T])
        hb = sb("hb", [P, 2, HC, T])
        ms_eps = sb("ms_eps", [P, PER])
        rms = sb("rms", [P, PER])
        diag = sb("diag", [P, PER, P])
        v = sb("v", [P, 2, T])
        tanh_v = sb("tanh_v", [P, 2, T])
        silu = sb("silu", [P, 2, T])
        silu_hi = sb("silu_hi", [P, HC, T], F32R)
        silu_lo = sb("silu_lo", [P, HC, T], F32R)
        x1 = sb("x1", [P, 2, T])
        stats2 = sb("stats2", [P, PER, 6])
        moments2 = sb("moments2", [P, PER, 2])
        var2 = sb("var2", [P, PER])
        rstd2 = sb("rstd2", [P, PER])
        shift2 = sb("shift2", [P, PER])
        norm2 = sb("norm2", [P, PER, P])
        h2_nodes = sb("h2_nodes", [P, PER, P])
        h2 = sb("h2", [P, 2, T])
        h2_hi = sb("h2_hi", [P, T], F32R)
        h2_lo = sb("h2_lo", [P, T], F32R)
        c1 = sb("c1", [P, PER, P])
        c1_hi = sb("c1_hi", [P, PER, PADDED], F32R)
        c1_lo = sb("c1_lo", [P, PER, PADDED], F32R)
        dist_l = sb("dist_l", [96, T])
        dist_r = sb("dist_r", [96, T])
        exp_dist = sb("exp_dist", [P, PER, P])
        kernel_a = sb("kernel_a", [P, PER, P])
        msg = sb("msg", [P, PER, P])
        nmp_hi = sb("nmp_hi", [P, T], F32R)
        nmp_lo = sb("nmp_lo", [P, T], F32R)
        conv_sum = sb("conv_sum", [P, T])
        xc = sb("xc", [P, T])
        xc_hi = sb("xc_hi", [P, T], F32R)
        xc_lo = sb("xc_lo", [P, T], F32R)
        tanh_r = sb("tanh_r", [P, T])
        tanh_z = sb("tanh_z", [P, T])
        gh_n = sb("gh_n", [P, T])
        r_gh = sb("r_gh", [P, T])
        n_in = sb("n_in", [P, T])
        n_gate = sb("n_gate", [P, T])
        h_minus_n = sb("h_minus_n", [P, T])
        x1_plus_n = sb("x1_plus_n", [P, T])
        z_part = sb("z_part", [P, T])
        out_sb = sb("out_sb", [P, T])

        bank = [ctx.enter_context(nc.psum_tensor(f"bank{i}", [P, T], F32)) for i in range(8)]
        conv2_ps = bank[0]
        conv1_ps = agg_ps = dist_ps = x1_nodes_ps = bank[1]
        seed_ps = w2_ps = ms_ps = bank[2]
        msg_ps = nmp_ps = h2_ps = bank[3]
        rms_ps = r_ps = bank[4]
        z_ps, hn_ps, in_ps = bank[5], bank[6], bank[7]
        w1_ps = [bank[3], bank[5], bank[6], bank[7]]

        raw_loaded = [sem(f"raw_loaded{i}") for i in range(3)]
        small_loaded = sem("small_loaded")
        split_hi, split_lo = sem("split_hi"), sem("split_lo")
        const_ready, eye_zeroed, eye_ready = sem("const_ready"), sem("eye_zeroed"), sem("eye_ready")
        prep, root_ready = sem("prep"), sem("root_ready")
        x_loaded = [sem(f"x_loaded{i}") for i in range(2)]
        adj_loaded = [sem(f"adj_loaded{i}") for i in range(2)]
        xT_loaded = [sem(f"xT_loaded{i}") for i in range(2)]
        mask_loaded = [sem(f"mask_loaded{i}") for i in range(2)]
        stats1_ready, moments1_ready, var1_ready = sem("stats1_ready"), sem("moments1_ready"), sem("var1_ready")
        rstd1_ready, shift1_ready, norm1_ready = sem("rstd1_ready"), sem("shift1_ready"), sem("norm1_ready")
        h1_ready, adj_eps_ready = sem("h1_ready"), sem("adj_eps_ready")
        agg_done, agg_hi_ready, agg_lo_ready = sem("agg_done"), sem("agg_hi_ready"), sem("agg_lo_ready")
        w1_done = [sem(f"w1_done{c}") for c in range(HC)]
        sq_ready = [sem(f"sq_ready{c}") for c in range(HC)]
        hb_ready = [sem(f"hb_ready{c}") for c in range(HC)]
        sq_pairs, sq_sum_ready = sem("sq_pairs"), sem("sq_sum_ready")
        ms_done, ms_eps_ready, rms_ready = sem("ms_done"), sem("ms_eps_ready"), sem("rms_ready")
        diag_ready, rms_done = sem("diag_ready"), sem("rms_done")
        v_ready = [sem(f"v_ready{c}") for c in range(HC)]
        tanh_ready = [sem(f"tanh_ready{c}") for c in range(HC)]
        silu_ready = [sem(f"silu_ready{c}") for c in range(HC)]
        silu_hi_ready = [sem(f"silu_hi_ready{c}") for c in range(HC)]
        silu_lo_ready = [sem(f"silu_lo_ready{c}") for c in range(HC)]
        w2_done, x1_ready, x1_nodes_done = sem("w2_done"), sem("x1_ready"), sem("x1_nodes_done")
        stats2_ready, moments2_ready, var2_ready = sem("stats2_ready"), sem("moments2_ready"), sem("var2_ready")
        rstd2_ready, shift2_ready, h2_nodes_ready = sem("rstd2_ready"), sem("shift2_ready"), sem("h2_nodes_ready")
        norm2_ready = sem("norm2_ready")
        h2_done, h2_ready, h2_hi_ready, h2_lo_ready = sem("h2_done"), sem("h2_ready"), sem("h2_hi_ready"), sem("h2_lo_ready")
        conv1_done, c1_ready, c1_hi_ready, c1_lo_ready = sem("conv1_done"), sem("c1_ready"), sem("c1_hi_ready"), sem("c1_lo_ready")
        seed_done, dist_ops_ready, dist_done, a_ready = sem("seed_done"), sem("dist_ops_ready"), sem("dist_done"), sem("a_ready")
        exp_ready = sem("exp_ready")
        msg_done, msg_sum_ready, msg_ready = sem("msg_done"), sem("msg_sum_ready"), sem("msg_ready")
        nmp_done, nmp_hi_ready, nmp_lo_ready = sem("nmp_done"), sem("nmp_hi_ready"), sem("nmp_lo_ready")
        conv2_done, conv_sum_ready, xc_ready = sem("conv2_done"), sem("conv_sum_ready"), sem("xc_ready")
        xc_hi_ready, xc_lo_ready = sem("xc_hi_ready"), sem("xc_lo_ready")
        r_done, z_done, hn_done, in_done = sem("r_done"), sem("z_done"), sem("hn_done"), sem("in_done")
        tanh_r_ready, tanh_z_ready, gh_n_ready = sem("tanh_r_ready"), sem("tanh_z_ready"), sem("gh_n_ready")
        r_gh_ready, n_in_ready, n_ready = sem("r_gh_ready"), sem("n_in_ready"), sem("n_ready")
        h_minus_n_ready, x1_plus_n_ready = sem("h_minus_n_ready"), sem("x1_plus_n_ready")
        z_part_ready, out_ready, stored = sem("z_part_ready"), sem("out_ready"), sem("stored")

        def need(eng, semaphore, groups):
            if type(groups) is int:
                if groups <= 0:
                    return
                groups = min(groups, NG)
            eng.wait_ge(semaphore, groups)

        def need_load(eng, semaphores, g, parity):
            eng.wait_ge(semaphores[parity], g * 8 + (16 - 8 * parity))

        def steps(eng, step, first=-3, last=NG):
            for t in range(first, LOOP_FIRST):
                step(t, t % 2)
            with eng.Fori(LOOP_FIRST, LOOP_END, 2) as t:
                for k in range(2):
                    step(t + k if k else t, (LOOP_FIRST + k) % 2)
            for t in range(LOOP_END, last + 1):
                step(t, t % 2)

        def has(t, lag):
            return type(t) is not int or 0 <= t + lag < NG

        def w(part, name, block):
            at = W_AT[name] + block * P
            return part[:, at:at + P]

        def bias(name):
            return vec[:, V_AT[name]:V_AT[name] + 1]

        def cols(name, n):
            return vec[:, V_AT[name]:V_AT[name] + n]

        def graph(j):
            return slice(j * P, (j + 1) * P)

        raw_loads = [("w1", "conv1", "msg", "hh", "w2"), ("ih", "conv2a"), ("conv2b",)]
        RAW_CUTS = [0, W_AT["ih"], W_AT["ih"] + 2176, W_TOTAL]
        assert max(b - a for a, b in zip(RAW_CUTS, RAW_CUTS[1:])) <= RAW and len(raw_loads) == 3

        block = ctx.enter_context(nc.Block())

        @block.sync
        def _(sp):
            def load_x(g, parity):
                need(sp, norm1_ready, g - 1)
                sp.dma_start(x_in[:, parity], x_nodes[g]).then_inc(x_loaded[parity], 16)
                need(sp, adj_eps_ready, g - 1)
                sp.dma_start(adj_in[:, parity], adj_t[g]).then_inc(adj_loaded[parity], 16)

            def load_xT(g, parity):
                need(sp, x1_ready, g - 1)
                sp.dma_start(xT_in[:, parity], x_feats[g]).then_inc(xT_loaded[parity], 16)

            def load_mask(g, parity):
                need(sp, a_ready, g - 1)
                sp.dma_start(mask_in[:, parity], adj_t[g]).then_inc(mask_loaded[parity], 16)

            def store(g):
                need(sp, out_ready, g + 1)
                sp.dma_start(out[g], out_sb[:]).then_inc(stored, 16)

            def load_raw(i):
                if i:
                    sp.wait_ge(split_hi, i)
                    sp.wait_ge(split_lo, i)
                a, b = RAW_CUTS[i:i + 2]
                sp.dma_start(w_raw[:, 0:b - a], weights[:, a:b]).then_inc(raw_loaded[i], 16)

            sp.dma_start(vec[:], vectors).then_inc(small_loaded, 16)
            sp.dma_start(eps_col[:], epsilon.partition_broadcast(P)).then_inc(small_loaded, 16)
            sp.dma_start(b_msg_sb[:], b_msg.partition_broadcast(P)).then_inc(small_loaded, 16)
            sp.dma_start(w_se_sb[:], w_se).then_inc(small_loaded, 16)
            load_x(0, 0)
            load_raw(0)
            load_x(1, 1)
            load_xT(0, 0)
            load_raw(1)
            load_xT(1, 1)
            load_raw(2)

            def step(t, parity):
                if has(t, 4) and not (type(t) is int and t + 4 < 2):
                    load_x(t + 4, parity)
                if has(t, 2) and not (type(t) is int and t + 2 < 2):
                    load_xT(t + 2, parity)
                if has(t, 1):
                    load_mask(t + 1, 1 - parity)
                if has(t, -1):
                    store(t - 1)

            for t in range(-2, 1):
                step(t, t % 2)
            with sp.Fori(1, 11, 2) as t:
                for k in range(2):
                    step(t + k if k else t, (1 + k) % 2)
            for t in range(11, NG + 1):
                step(t, t % 2)
            sp.wait_ge(stored, 16 * NG)

        @block.tensor
        def _(pe):
            def exact(out_ps, name, block_, hi, lo, first, last):
                nc.tensor.matmul(out_ps, w(w_hi, name, block_), hi, start=first, stop=False)
                nc.tensor.matmul(out_ps, w(w_hi, name, block_), lo, start=False, stop=False)
                return nc.tensor.matmul(out_ps, w(w_lo, name, block_), hi, start=False, stop=last)

            def conv1(g):
                need(pe, h2_hi_ready, g + 1)
                need(pe, h2_lo_ready, g + 1)
                exact(conv1_ps[:], "conv1", 0, h2_hi[:], h2_lo[:], True, True).then_inc(conv1_done, 1)

            def seeds(g):
                need(pe, ms_eps_ready, g + 2)
                need(pe, h2_ready, g + 1)
                h = h2[:, g_parity(g)]
                nc.tensor.matmul(seed_ps[:], w_se_sb[:], h, start=True, stop=True).then_inc(seed_done, 1)

            def messages(g):
                for j in range(PER):
                    ps = msg_ps[:, graph(j)]
                    nc.tensor.matmul(ps, h2_hi[:, graph(j)], w(w_hi, "msg", 0), start=True, stop=False)
                    nc.tensor.matmul(ps, h2_hi[:, graph(j)], w(w_lo, "msg", 0), start=False, stop=False)
                    last = nc.tensor.matmul(ps, h2_lo[:, graph(j)], w(w_hi, "msg", 0), start=False, stop=True)
                last.then_inc(msg_done, 1)

            def aggregate(g):
                need(pe, h1_ready, g + 1)
                need(pe, adj_eps_ready, g + 1)
                need(pe, c1_ready, g - 1)
                for j in range(PER):
                    last = nc.tensor.matmul(agg_ps[:, graph(j)], h1[:, j], adj_eps[:, j], start=True, stop=True)
                last.then_inc(agg_done, 1)

            def rms_rows(g):
                need(pe, diag_ready, g + 1)
                need(pe, tanh_r_ready, g - 1)
                nc.tensor.matmul(rms_ps[:], ones[:], diag[:].rearrange("p g n -> p (g n)"),
                                 start=True, stop=True).then_inc(rms_done, 1)

            def w1(g):
                need(pe, agg_hi_ready, g + 1)
                need(pe, agg_lo_ready, g + 1)
                for c, (semaphore, groups) in enumerate(((msg_sum_ready, g - 1), (tanh_z_ready, g - 2),
                                                         (gh_n_ready, g - 2), (n_in_ready, g - 2))):
                    need(pe, semaphore, groups)
                    exact(w1_ps[c][:], "w1", c, agg_hi[:], agg_lo[:], True, True).then_inc(w1_done[c], 1)

            def distances(g):
                need(pe, dist_ops_ready, g + 1)
                need(pe, agg_hi_ready, g + 3)
                need(pe, agg_lo_ready, g + 3)
                for j in range(PER):
                    last = nc.tensor.matmul(dist_ps[:, graph(j)], dist_l[:, graph(j)], dist_r[:, graph(j)],
                                            start=True, stop=True)
                last.then_inc(dist_done, 1)

            taps = sorted(range(TAPS), key=lambda k: abs(k - HALF))
            cuts = [0, 6, 12, 14, TAPS]

            def conv2(g, part):
                if part == 0:
                    need(pe, c1_hi_ready, g + 1)
                    need(pe, c1_lo_ready, g + 1)
                    need(pe, conv_sum_ready, g)
                ps = conv2_ps[:].rearrange("p (g n) -> p g n", n=P)
                for k in taps[cuts[part]:cuts[part + 1]]:
                    s = k - HALF
                    a, b = max(0, -s) & ~1, P - (max(0, s) & ~1)
                    o, hi, lo = (ps[:, :, a:b], c1_hi[:, :, a + s + 1:b + s + 1], c1_lo[:, :, a + s + 1:b + s + 1])
                    last = exact(o, "conv2", k, hi, lo, k == taps[0], k == taps[-1])
                if part == 3:
                    last.then_inc(conv2_done, 1)

            def w2(g, c):
                if c == 0:
                    need(pe, dist_ops_ready, g)
                need(pe, silu_hi_ready[c], g + 1)
                need(pe, silu_lo_ready[c], g + 1)
                last = exact(w2_ps[:], "w2", c, silu_hi[:, c], silu_lo[:, c], c == 0, c == HC - 1)
                if c == HC - 1:
                    last.then_inc(w2_done, 1)

            def gather(g):
                need(pe, a_ready, g + 1)
                need(pe, msg_ready, g + 1)
                need(pe, sq_ready[0], g + 3)
                need(pe, hb_ready[0], g + 3)
                for j in range(PER):
                    last = nc.tensor.matmul(nmp_ps[:, graph(j)], msg[:, j], kernel_a[:, j], start=True, stop=True)
                last.then_inc(nmp_done, 1)

            def x1_by_nodes(g, parity):
                need(pe, x1_ready, g + 1)
                need(pe, exp_ready, g)
                for j in range(PER):
                    last = nc.tensor.transpose(x1_nodes_ps[:, graph(j)], x1[:, parity, graph(j)], eye[:])
                last.then_inc(x1_nodes_done, 1)

            def mean_squares(g):
                need(pe, sq_sum_ready, g + 1)
                need(pe, x1_ready, g)
                for j in range(PER):
                    last = nc.tensor.matmul(ms_ps[:, j:j + 1], sq[:, 0, graph(j)], mean_col[:], start=True, stop=True)
                last.then_inc(ms_done, 1)

            def h2_by_features(g):
                need(pe, h2_nodes_ready, g + 1)
                need(pe, nmp_hi_ready, g)
                need(pe, nmp_lo_ready, g)
                for j in range(PER):
                    last = nc.tensor.transpose(h2_ps[:, graph(j)], h2_nodes[:, j], eye[:])
                last.then_inc(h2_done, 1)

            def gates_early(g):
                need(pe, nmp_hi_ready, g + 1)
                need(pe, nmp_lo_ready, g + 1)
                need(pe, v_ready[HC - 1], g + 2)
                exact(r_ps[:], "hh", 0, h2_hi[:], h2_lo[:], True, False)
                exact(r_ps[:], "ih", 3, nmp_hi[:], nmp_lo[:], False, False)
                for c in range(1, HC):
                    need(pe, sq_ready[c], g + 3)
                    need(pe, hb_ready[c], g + 3)
                exact(z_ps[:], "hh", 1, h2_hi[:], h2_lo[:], True, False)
                exact(z_ps[:], "ih", 4, nmp_hi[:], nmp_lo[:], False, False)
                exact(hn_ps[:], "hh", 2, h2_hi[:], h2_lo[:], True, True).then_inc(hn_done, 1)
                exact(in_ps[:], "ih", 5, nmp_hi[:], nmp_lo[:], True, False)

            def gates_late(g):
                need(pe, xc_hi_ready, g + 1)
                need(pe, xc_lo_ready, g + 1)
                exact(r_ps[:], "ih", 0, xc_hi[:], xc_lo[:], False, True).then_inc(r_done, 1)
                exact(z_ps[:], "ih", 1, xc_hi[:], xc_lo[:], False, True).then_inc(z_done, 1)
                exact(in_ps[:], "ih", 2, xc_hi[:], xc_lo[:], False, True).then_inc(in_done, 1)

            now = {}

            def g_parity(g):
                return now["parity"]

            def step(t, parity):
                now["parity"] = parity
                if has(t, 0):
                    if type(t) is int and t == 0:
                        pe.wait_ge(split_lo, 3)
                    conv1(t)
                    seeds(t)
                    messages(t)
                if has(t, 2):
                    if type(t) is int and t == -2:
                        pe.wait_ge(eye_ready, 1)
                        pe.wait_ge(const_ready, 1)
                        pe.wait_ge(split_hi, 1)
                        pe.wait_ge(split_lo, 1)
                        pe.wait_ge(small_loaded, 64)
                    aggregate(t + 2)
                if has(t, 1):
                    rms_rows(t + 1)
                if has(t, 0):
                    conv2(t, 0)
                if has(t, 2):
                    w1(t + 2)
                if has(t, 0):
                    distances(t)
                    conv2(t, 1)
                if has(t, 1):
                    w2(t + 1, 0)
                    w2(t + 1, 1)
                if has(t, 0):
                    gather(t)
                if has(t, 1):
                    w2(t + 1, 2)
                    w2(t + 1, 3)
                if has(t, 0):
                    conv2(t, 2)
                if has(t, 1):
                    x1_by_nodes(t + 1, 1 - parity)
                if has(t, 2):
                    mean_squares(t + 2)
                if has(t, 0):
                    conv2(t, 3)
                    gates_early(t)
                if has(t, 1):
                    h2_by_features(t + 1)
                if has(t, 0):
                    gates_late(t)

            steps(pe, step)

        @block.scalar
        def _(act):
            act.wait_ge(prep, 1)
            nc.scalar.activation(bn_root[:], bn_root[:], ACT.Sqrt).then_inc(root_ready, 1)

            def split_high(i):
                act.wait_ge(raw_loaded[i], 16)
                a, b = RAW_CUTS[i:i + 2]
                nc.scalar.copy(w_hi[:, a:b], w_raw[:, 0:b - a]).then_inc(split_hi, 1)

            split_high(0)
            act.wait_ge(prep, 9)

            def r_and_z(g):
                need(act, r_done, g + 1)
                need(act, r_gh_ready, g)
                nc.scalar.activation(tanh_r[:], r_ps[:], ACT.Tanh, bias=gate_bias[:, 0:1], scale=0.5).then_inc(tanh_r_ready, 1)
                need(act, hn_done, g + 1)
                nc.scalar.activation(gh_n[:], hn_ps[:], ACT.Identity, bias=bias("bhh_n")).then_inc(gh_n_ready, 1)
                need(act, z_done, g + 1)
                need(act, z_part_ready, g)
                nc.scalar.activation(tanh_z[:], z_ps[:], ACT.Tanh, bias=gate_bias[:, 1:2], scale=0.5).then_inc(tanh_z_ready, 1)

            def n_of(g):
                need(act, n_in_ready, g + 1)
                need(act, h_minus_n_ready, g)
                need(act, x1_plus_n_ready, g)
                nc.scalar.activation(n_gate[:], n_in[:], ACT.Tanh, bias=bias("bih_n")).then_inc(n_ready, 1)

            def conv1_relu(g):
                need(act, conv1_done, g + 1)
                need(act, c1_hi_ready, g)
                need(act, c1_lo_ready, g)
                nc.scalar.activation(c1[:].rearrange("p g n -> p (g n)"), conv1_ps[:], ACT.Relu, bias=bn_bias[:, 0:1],
                                     scale=bn_scale[:, 0:1]).then_inc(c1_ready, 1)

            def distance_operands(g):
                need(act, seed_done, g + 1)
                need(act, dist_done, g)
                nc.scalar.activation(dist_l[0:32], seed_ps[0:32], ACT.Identity, bias=bias("bse")[0:32])
                nc.scalar.activation(dist_r[0:32], seed_ps[0:32], ACT.Identity, bias=bias("bse")[0:32])
                nc.scalar.activation(dist_l[32:64], seed_ps[32:64], ACT.Square, bias=bias("bse")[32:64])
                nc.scalar.activation(dist_r[64:96], seed_ps[64:96], ACT.Square, bias=bias("bse")[64:96]).then_inc(dist_ops_ready, 1)

            def aggregate_high(g):
                need(act, agg_done, g + 1)
                need(act, w1_done[HC - 1], g)
                nc.scalar.copy(agg_hi[:], agg_ps[:]).then_inc(agg_hi_ready, 1)

            def silu_tanh(g):
                for c in range(HC):
                    need(act, v_ready[c], g + 1)
                    need(act, silu_ready[(c + 2) % HC], g + (1 if c >= 2 else 0))
                    nc.scalar.activation(tanh_v[:, c % 2], v[:, c % 2], ACT.Tanh).then_inc(tanh_ready[c], 1)

            def hidden(g, parity):
                for c in range(HC):
                    need(act, w1_done[c], g + 1)
                    if c == 0:
                        need(act, ms_done, g)
                        need(act, v_ready[HC - 1], g - 1)
                    nc.scalar.activation(sq[:, c], w1_ps[c][:], ACT.Square, bias=bias(f"b1_{c}")).then_inc(sq_ready[c], 1)
                    nc.scalar.activation(hb[:, parity, c], w1_ps[c][:], ACT.Identity, bias=hb_bias[:, c:c + 1],
                                         scale=bias(f"rms_{c}")).then_inc(hb_ready[c], 1)

            def exponential(g):
                need(act, dist_done, g + 1)
                need(act, a_ready, g)
                nc.scalar.activation(exp_dist[:].rearrange("p g n -> p (g n)"), dist_ps[:], ACT.Exp, scale=2.0).then_inc(exp_ready, 1)

            def gathered_high(g):
                need(act, nmp_done, g + 1)
                need(act, in_done, g)
                nc.scalar.copy(nmp_hi[:], nmp_ps[:]).then_inc(nmp_hi_ready, 1)

            def h2_full(g, parity):
                need(act, h2_done, g + 1)
                need(act, h_minus_n_ready, g - 1)
                nc.scalar.copy(h2[:, parity], h2_ps[:]).then_inc(h2_ready, 1)

            def step(t, parity):
                if has(t, -1):
                    r_and_z(t - 1)
                if has(t, 0):
                    conv1_relu(t)
                if has(t, -1):
                    n_of(t - 1)
                if has(t, 0):
                    distance_operands(t)
                if has(t, 2):
                    aggregate_high(t + 2)
                if type(t) is int and t == -2:
                    split_high(1)
                if has(t, 1):
                    silu_tanh(t + 1)
                if type(t) is int and t == -1:
                    split_high(2)
                if has(t, 2):
                    hidden(t + 2, parity)
                if has(t, 0):
                    exponential(t)
                    gathered_high(t)
                if has(t, 1):
                    h2_full(t + 1, 1 - parity)

            steps(act, step)

        @block.vector
        def _(dve):
            done = [0]

            def chained(ins):
                done[0] += 1
                ins.then_inc(prep, 1)
                dve.wait_ge(prep, done[0])

            for side in (0, P + 1):
                nc.vector.memset(c1_hi[:, :, side:side + 1].bitcast(F32), 0.0)
                nc.vector.memset(c1_lo[:, :, side:side + 1].bitcast(F32), 0.0)
            nc.vector.memset(dist_l[64:96], -0.5)
            nc.vector.memset(dist_r[32:64], -0.5)
            nc.vector.memset(mean_col[:], 1.0 / (HC * P))
            nc.vector.memset(minus_half[:], -0.5)
            nc.vector.memset(ones[:], 1.0).then_inc(const_ready, 1)
            dve.wait_ge(small_loaded, 64)
            chained(nc.vector.tensor_scalar(bn_root[:], cols("bn1_v", 2), BN_EPS, None, ALU.add))
            chained(nc.vector.tensor_scalar(cols("rms_0", HC), cols("rms_0", HC), 0.5, None, ALU.mult))
            chained(nc.vector.tensor_tensor(hb_bias[:], cols("b1_0", HC), cols("rms_0", HC), ALU.mult))
            chained(nc.vector.tensor_tensor(gate_sum[:], cols("bih_r", 2), cols("bhh_r", 2), ALU.add))
            chained(nc.vector.tensor_scalar(gate_bias[:], gate_sum[:], 0.5, None, ALU.mult))
            dve.wait_ge(root_ready, 1)
            chained(nc.vector.reciprocal(bn_inv[:], bn_root[:]))
            chained(nc.vector.tensor_tensor(bn_scale[:], bn_inv[:], cols("bn1_g", 2), ALU.mult))
            chained(nc.vector.tensor_tensor(bn_ms[:], bn_scale[:], cols("bn1_m", 2), ALU.mult))
            chained(nc.vector.tensor_tensor(bn_bias[:], cols("bn1_b", 2), bn_ms[:], ALU.subtract))

            def split_low(i):
                dve.wait_ge(split_hi, i + 1)
                a, b = RAW_CUTS[i:i + 2]
                nc.vector.tensor_tensor(w_lo[:, a:b], w_raw[:, 0:b - a], w_hi[:, a:b].bitcast(F32),
                                        ALU.subtract).then_inc(split_lo, 1)

            def reset_and_input(g):
                need(dve, tanh_r_ready, g + 1)
                need(dve, gh_n_ready, g + 1)
                need(dve, n_in_ready, g)
                nc.vector.scalar_tensor_tensor(r_gh[:], tanh_r[:], 1.0, gh_n[:], ALU.add, ALU.mult).then_inc(r_gh_ready, 1)
                need(dve, r_gh_ready, g + 1)
                need(dve, in_done, g + 1)
                need(dve, n_ready, g)
                nc.vector.scalar_tensor_tensor(n_in[:], r_gh[:], 0.5, in_ps[:], ALU.mult, ALU.add).then_inc(n_in_ready, 1)

            def conv1_split(g):
                need(dve, c1_ready, g + 1)
                need(dve, conv2_done, g)
                nc.vector.tensor_copy(c1_hi[:, :, 1:P + 1], c1[:]).then_inc(c1_hi_ready, 1)
                need(dve, c1_hi_ready, g + 1)
                nc.vector.tensor_tensor(c1_lo[:, :, 1:P + 1], c1[:], c1_hi[:, :, 1:P + 1].bitcast(F32),
                                        ALU.subtract).then_inc(c1_lo_ready, 1)

            def message_relu(g):
                need(dve, msg_done, g + 1)
                need(dve, nmp_done, g)
                nc.vector.tensor_tensor(msg[:], msg_ps[:].rearrange("p (g n) -> p g n", n=P), b_msg_sb[:],
                                        ALU.add).then_inc(msg_sum_ready, 1)
                need(dve, msg_sum_ready, g + 1)
                nc.vector.tensor_scalar(msg[:], msg[:], 0.0, None, ALU.max).then_inc(msg_ready, 1)

            def aggregate_low(g):
                need(dve, agg_hi_ready, g + 1)
                nc.vector.tensor_tensor(agg_lo[:], agg_ps[:], agg_hi[:].bitcast(F32), ALU.subtract).then_inc(agg_lo_ready, 1)

            def v_of(g, parity, c):
                if c == 0:
                    need(dve, rms_done, g + 1)
                need(dve, hb_ready[c], g + 1)
                need(dve, silu_ready[(c + 2) % HC], g + (1 if c >= 2 else 0))
                nc.vector.tensor_tensor(v[:, c % 2], rms_ps[:], hb[:, parity, c], ALU.mult).then_inc(v_ready[c], 1)

            def silu_of(g, c):
                need(dve, tanh_ready[c], g + 1)
                need(dve, silu_lo_ready[(c + 2) % HC], g + (1 if c >= 2 else 0))
                nc.vector.scalar_tensor_tensor(silu[:, c % 2], tanh_v[:, c % 2], 1.0, v[:, c % 2], ALU.add,
                                               ALU.mult).then_inc(silu_ready[c], 1)
                need(dve, silu_ready[c], g + 1)
                need(dve, w2_done, g)
                nc.vector.tensor_copy(silu_hi[:, c], silu[:, c % 2]).then_inc(silu_hi_ready[c], 1)

            def state(g):
                need(dve, h_minus_n_ready, g + 1)
                need(dve, tanh_z_ready, g + 1)
                need(dve, out_ready, g)
                nc.vector.scalar_tensor_tensor(z_part[:], tanh_z[:], 1.0, h_minus_n[:], ALU.add, ALU.mult).then_inc(z_part_ready, 1)
                need(dve, z_part_ready, g + 1)
                need(dve, x1_plus_n_ready, g + 1)
                dve.wait_ge(stored, g * 16) if type(g) is not int or g > 0 else None
                nc.vector.scalar_tensor_tensor(out_sb[:], z_part[:], 0.5, x1_plus_n[:], ALU.mult, ALU.add).then_inc(out_ready, 1)

            def layernorm1_stats(g, parity):
                need_load(dve, x_loaded, g, parity)
                for j in range(PER):
                    last = nc.vector.bn_stats(stats1[:, j], x_in[:, parity, j])
                last.then_inc(stats1_ready, 1)

            def layernorm1_moments(g):
                need(dve, rstd1_ready, g)
                need(dve, stats1_ready, g + 1)
                nc.vector.memset(var1[:], 0.0)
                for j in range(PER):
                    last = nc.vector.bn_aggr(moments1[:, j], stats1[:, j])
                last.then_inc(moments1_ready, 1)
                need(dve, moments1_ready, g + 1)
                nc.vector.tensor_scalar(var1[:], moments1[:, :, 1], LN_EPS, None, ALU.add).then_inc(var1_ready, 1)

            def layernorm1_apply(g, parity):
                need(dve, rstd1_ready, g + 1)
                nc.vector.scalar_tensor_tensor(shift1[:], moments1[:, :, 0], -1.0, rstd1[:], ALU.mult, ALU.mult).then_inc(shift1_ready, 1)
                need(dve, shift1_ready, g + 1)
                need(dve, h1_ready, g)
                for j in range(PER):
                    last = nc.vector.tensor_scalar(norm1[:, j], x_in[:, parity, j], rstd1[:, j:j + 1], shift1[:, j:j + 1],
                                                   ALU.mult, ALU.add)
                last.then_inc(norm1_ready, 1)
                need(dve, norm1_ready, g + 1)
                need(dve, agg_done, g)
                nc.vector.tensor_scalar(h1[:], norm1[:], 0.0, None, ALU.max).then_inc(h1_ready, 1)

            def gathered_low(g):
                need(dve, nmp_hi_ready, g + 1)
                nc.vector.tensor_tensor(nmp_lo[:], nmp_ps[:], nmp_hi[:].bitcast(F32), ALU.subtract).then_inc(nmp_lo_ready, 1)

            def residual1(g, parity):
                need(dve, w2_done, g + 1)
                need_load(dve, xT_loaded, g, parity)
                need(dve, x1_plus_n_ready, g - 1)
                nc.vector.scalar_tensor_tensor(x1[:, parity], w2_ps[:], bias("b2"), xT_in[:, parity], ALU.add,
                                               ALU.add).then_inc(x1_ready, 1)

            def mean_square_eps(g):
                need(dve, ms_done, g + 1)
                need(dve, rms_ready, g)
                nc.vector.tensor_scalar(ms_eps[:], ms_ps[:, 0:PER], RMS_EPS, None, ALU.add).then_inc(ms_eps_ready, 1)

            def layernorm2_stats(g):
                need(dve, x1_nodes_done, g + 1)
                for j in range(PER):
                    last = nc.vector.bn_stats(stats2[:, j], x1_nodes_ps[:, graph(j)])
                last.then_inc(stats2_ready, 1)

            def layernorm2_moments(g):
                need(dve, rstd2_ready, g)
                need(dve, stats2_ready, g + 1)
                nc.vector.memset(var2[:], 0.0)
                for j in range(PER):
                    last = nc.vector.bn_aggr(moments2[:, j], stats2[:, j])
                last.then_inc(moments2_ready, 1)
                need(dve, moments2_ready, g + 1)
                nc.vector.tensor_scalar(var2[:], moments2[:, :, 1], LN_EPS, None, ALU.add).then_inc(var2_ready, 1)

            def layernorm2_apply(g):
                need(dve, rstd2_ready, g + 1)
                nc.vector.scalar_tensor_tensor(shift2[:], moments2[:, :, 0], -1.0, rstd2[:], ALU.mult, ALU.mult).then_inc(shift2_ready, 1)
                need(dve, shift2_ready, g + 1)
                need(dve, h2_done, g)
                for j in range(PER):
                    last = nc.vector.tensor_scalar(norm2[:, j], x1_nodes_ps[:, graph(j)], rstd2[:, j:j + 1],
                                                   shift2[:, j:j + 1], ALU.mult, ALU.add)
                last.then_inc(norm2_ready, 1)
                need(dve, norm2_ready, g + 1)
                nc.vector.tensor_scalar(h2_nodes[:], norm2[:], 0.0, None, ALU.max).then_inc(h2_nodes_ready, 1)

            def rms_diagonal(g):
                need(dve, rms_ready, g + 1)
                need(dve, rms_done, g)
                for j in range(PER):
                    last = nc.vector.tensor_scalar(diag[:, j], eye[:], rms[:, j:j + 1], None, ALU.mult)
                last.then_inc(diag_ready, 1)

            def conv2_relu(g, parity):
                need(dve, conv2_done, g + 1)
                need(dve, h2_ready, g + 1)
                need(dve, xc_ready, g)
                nc.vector.scalar_tensor_tensor(conv_sum[:], conv2_ps[:], bn_scale[:, 1:2], h2[:, parity], ALU.mult,
                                               ALU.add).then_inc(conv_sum_ready, 1)
                need(dve, conv_sum_ready, g + 1)
                need(dve, xc_lo_ready, g)
                nc.vector.tensor_scalar(xc[:], conv_sum[:], bn_bias[:, 1:2], 0.0, ALU.add, ALU.max).then_inc(xc_ready, 1)
                need(dve, xc_ready, g + 1)
                need(dve, in_done, g)
                nc.vector.tensor_copy(xc_hi[:], xc[:]).then_inc(xc_hi_ready, 1)
                need(dve, xc_hi_ready, g + 1)
                nc.vector.tensor_tensor(xc_lo[:], xc[:], xc_hi[:].bitcast(F32), ALU.subtract).then_inc(xc_lo_ready, 1)

            def h2_split(g, parity):
                need(dve, h2_ready, g + 1)
                need(dve, hn_done, g)
                nc.vector.tensor_copy(h2_hi[:], h2[:, parity]).then_inc(h2_hi_ready, 1)
                need(dve, h2_hi_ready, g + 1)
                nc.vector.tensor_tensor(h2_lo[:], h2[:, parity], h2_hi[:].bitcast(F32), ALU.subtract).then_inc(h2_lo_ready, 1)

            def step(t, parity):
                if type(t) is int and t == -3:
                    split_low(0)
                if type(t) is int and t == -2:
                    dve.wait_ge(eye_ready, 1)
                if has(t, -1):
                    reset_and_input(t - 1)
                if has(t, 0):
                    conv1_split(t)
                    message_relu(t)
                if has(t, 2):
                    aggregate_low(t + 2)
                if type(t) is int and t == -2:
                    split_low(1)
                if has(t, 1):
                    v_of(t + 1, 1 - parity, 0)
                    v_of(t + 1, 1 - parity, 1)
                    silu_of(t + 1, 0)
                    v_of(t + 1, 1 - parity, 2)
                    silu_of(t + 1, 1)
                    v_of(t + 1, 1 - parity, 3)
                    silu_of(t + 1, 2)
                    silu_of(t + 1, 3)
                if type(t) is int and t == -1:
                    split_low(2)
                if has(t, 3):
                    layernorm1_stats(t + 3, 1 - parity)
                    layernorm1_moments(t + 3)
                if has(t, -1):
                    state(t - 1)
                if has(t, 3):
                    layernorm1_apply(t + 3, 1 - parity)
                if has(t, 0):
                    gathered_low(t)
                if has(t, 1):
                    residual1(t + 1, 1 - parity)
                if has(t, 2):
                    mean_square_eps(t + 2)
                if has(t, 1):
                    layernorm2_stats(t + 1)
                    layernorm2_moments(t + 1)
                if has(t, 2):
                    rms_diagonal(t + 2)
                if has(t, 0):
                    conv2_relu(t, parity)
                if has(t, 1):
                    layernorm2_apply(t + 1)
                    h2_split(t + 1, 1 - parity)

            steps(dve, step)

        @block.gpsimd
        def _(pool):
            nc.gpsimd.memset(eye[:], 0.0).then_inc(eye_zeroed, 1)
            pool.wait_ge(eye_zeroed, 1)
            nc.gpsimd.affine_select(out=eye[:], in_=eye[:], compare_op=ALU.not_equal, fill=1.0, base=0,
                                    pattern=[[-1, P]], channel_multiplier=1).then_inc(eye_ready, 1)
            pool.wait_ge(eye_ready, 1)
            pool.wait_ge(small_loaded, 64)
            for j in range(PER):
                last = nc.gpsimd.tensor_scalar(eps_eye[:, j], eye[:], eps_col[:, 0:1], None, ALU.mult)
            last.then_inc(eye_zeroed, 1)
            pool.wait_ge(eye_zeroed, 2)
            pool.wait_ge(const_ready, 1)

            def blend_inputs(g, parity):
                need(pool, n_ready, g + 1)
                need(pool, z_part_ready, g)
                nc.gpsimd.tensor_tensor(h_minus_n[:], h2[:, parity], n_gate[:], ALU.subtract).then_inc(h_minus_n_ready, 1)
                need(pool, out_ready, g)
                nc.gpsimd.tensor_tensor(x1_plus_n[:], x1[:, parity], n_gate[:], ALU.add).then_inc(x1_plus_n_ready, 1)

            def silu_low(g):
                for c in range(HC):
                    need(pool, silu_hi_ready[c], g + 1)
                    nc.gpsimd.tensor_tensor(silu_lo[:, c], silu[:, c % 2], silu_hi[:, c].bitcast(F32),
                                            ALU.subtract).then_inc(silu_lo_ready[c], 1)

            def square_sum(g):
                need(pool, sq_ready[1], g + 1)
                nc.gpsimd.tensor_tensor(sq[:, 0], sq[:, 0], sq[:, 1], ALU.add)
                need(pool, sq_ready[3], g + 1)
                nc.gpsimd.tensor_tensor(sq[:, 2], sq[:, 2], sq[:, 3], ALU.add).then_inc(sq_pairs, 1)
                need(pool, sq_pairs, g + 1)
                nc.gpsimd.tensor_tensor(sq[:, 0], sq[:, 0], sq[:, 2], ALU.add).then_inc(sq_sum_ready, 1)

            def rstd1_of(g):
                need(pool, var1_ready, g + 1)
                need(pool, norm1_ready, g)
                nc.gpsimd.tensor_tensor(rstd1[:], var1[:], minus_half[:], ALU.pow).then_inc(rstd1_ready, 1)

            def adjacency_eps(g, parity):
                need_load(pool, adj_loaded, g, parity)
                need(pool, agg_done, g)
                nc.gpsimd.tensor_tensor(adj_eps[:], adj_in[:, parity], eps_eye[:], ALU.add).then_inc(adj_eps_ready, 1)

            def masked(g, parity):
                need(pool, exp_ready, g + 1)
                need_load(pool, mask_loaded, g, parity)
                need(pool, nmp_done, g)
                nc.gpsimd.tensor_tensor(kernel_a[:], exp_dist[:], mask_in[:, parity], ALU.mult).then_inc(a_ready, 1)

            def rms_of(g):
                need(pool, ms_eps_ready, g + 1)
                need(pool, diag_ready, g)
                nc.gpsimd.tensor_tensor(rms[:], ms_eps[:], minus_half[:], ALU.pow).then_inc(rms_ready, 1)

            def rstd2_of(g):
                need(pool, var2_ready, g + 1)
                need(pool, h2_nodes_ready, g)
                nc.gpsimd.tensor_tensor(rstd2[:], var2[:], minus_half[:], ALU.pow).then_inc(rstd2_ready, 1)

            def step(t, parity):
                if has(t, -1):
                    blend_inputs(t - 1, 1 - parity)
                if has(t, 1):
                    silu_low(t + 1)
                if has(t, 3):
                    rstd1_of(t + 3)
                if has(t, 2):
                    square_sum(t + 2)
                if has(t, 0):
                    masked(t, parity)
                if has(t, 3):
                    adjacency_eps(t + 3, 1 - parity)
                if has(t, 2):
                    rms_of(t + 2)
                if has(t, 1):
                    rstd2_of(t + 1)

            steps(pool, step)


def kernel(x, adj, **p):
    import concourse.bacc as bacc
    from concourse.bass_utils import run_bass_kernel_spmd

    def grouped(a, order):
        a = np.asarray(a).reshape(NG, PER, P, P).transpose(0, *(1 + k for k in order))
        return np.ascontiguousarray(a.reshape(NG, P, T))

    arr = {k: np.asarray(a) for k, a in p.items()}
    g1 = lambda name: arr["L1_gnn_" + name]
    parts = {
        "w1": arr["L0_gnn_W1"],
        "conv1": g1("conv1_w")[:, :, 0].T,
        "msg": g1("w_msg").T,
        "hh": g1("w_hh").T,
        "w2": arr["L0_gnn_W2"].reshape(HC, P, P).transpose(1, 0, 2).reshape(P, HC * P),
        "ih": g1("w_ih").reshape(3 * P, 2, P).transpose(2, 1, 0).reshape(P, 6 * P),
        "conv2": g1("conv2_w").transpose(1, 2, 0).reshape(P, TAPS * P),
    }
    weights = np.concatenate([parts[n] for n in W_COLS], axis=1)
    w_se = np.zeros((P, P), np.float32)
    bse = np.zeros(P, np.float32)
    for q in range(3):
        w_se[:, 32 * q:32 * q + SEEDS] = g1("w_se").T
        bse[32 * q:32 * q + SEEDS] = g1("b_se")
    vectors = {"bse": bse, "b2": arr["L0_gnn_b2"]}
    for c in range(HC):
        vectors[f"b1_{c}"] = arr["L0_gnn_b1"][c * P:(c + 1) * P]
        vectors[f"rms_{c}"] = arr["L0_gnn_rms_weight"][c * P:(c + 1) * P]
    for n in ("bn1", "bn2"):
        for k in "gbmv":
            vectors[f"{n}_{k}"] = g1(f"{n}_{k}")
    for i, gate in enumerate("rzn"):
        vectors[f"bih_{gate}"] = g1("b_ih")[i * P:(i + 1) * P]
        vectors[f"bhh_{gate}"] = g1("b_hh")[i * P:(i + 1) * P]
    inputs = {
        "x_nodes": grouped(x, (1, 0, 2)),
        "x_feats": grouped(x, (2, 0, 1)),
        "adj_t": grouped(adj, (2, 0, 1)),
        "weights": np.ascontiguousarray(weights),
        "w_se": w_se,
        "vectors": np.ascontiguousarray(np.stack([vectors[n] for n in V_NAMES], axis=1)),
        "b_msg": np.ascontiguousarray(np.tile(g1("b_msg"), PER)),
        "epsilon": arr["L0_gnn_epsilon"].reshape(1),
    }
    nc = bacc.Bacc("TRN2", target_bir_lowering=False, num_devices=1)
    args = [nc.dram_tensor(n, a.shape, mybir.dt.from_np(a.dtype), kind="ExternalInput").ap() for n, a in inputs.items()]
    out = nc.dram_tensor("out", (NG, P, T), F32, kind="ExternalOutput").ap()
    build(nc, *args, out)
    r = run_bass_kernel_spmd(nc, [inputs], core_ids=[0])
    got = r.results[0]["out"]
    return got.reshape(NG, P, PER, P).transpose(0, 2, 3, 1).reshape(GRAPHS, P, P)
```

```python
from contextlib import ExitStack

import numpy as np

import concourse.bass as bass
from concourse import mybir
from concourse.alu_op_type import AluOpType as ALU

F32 = mybir.dt.float32
F32R = mybir.dt.float32r
ACT = mybir.ActivationFunctionType

P = 128
GRAPHS = 64
PER = 4
T = PER * P
NG = GRAPHS // PER
HC = 4
TAPS = 17
HALF = TAPS // 2
PH = P // 2
PADDED = PH + 4
P1_COLS = PH + 2
LN_EPS, RMS_EPS, BN_EPS = 1e-5, 1e-6, 1e-5
SEEDS = 3
LOOP_FIRST, LOOP_END = 2, 12

W_COLS = {"w1": HC * P, "conv1": P, "msg": P, "se": P, "hh": 3 * P, "w2": HC * P, "ih": 6 * P, "conv2": TAPS * P,
          "conv2_pairs": (TAPS - 1) * P // 2}
W_AT = {}
for _name in W_COLS:
    W_AT[_name] = sum(W_COLS[n] for n in W_AT)
W_TOTAL = sum(W_COLS.values())

V_NAMES = (["b1_0", "b1_1", "b1_2", "b1_3", "rms_0", "rms_1", "rms_2", "rms_3", "b2", "bse",
            "bn1_g", "bn2_g", "bn1_b", "bn2_b", "bn1_m", "bn2_m", "bn1_v", "bn2_v",
            "bih_r", "bih_z", "bih_n", "bhh_r", "bhh_z", "bhh_n"])
V_AT = {n: i for i, n in enumerate(V_NAMES)}


def build(nc, x_nodes, x_feats, adj_t, weights, vectors, b_msg, epsilon, out):
    with ExitStack() as ctx:
        def sb(name, shape, dt=F32):
            return ctx.enter_context(nc.sbuf_tensor(name, shape, dt))

        def sem(name):
            return ctx.enter_context(nc.semaphore(name))

        w_hi = sb("w_hi", [P, W_TOTAL], F32R)
        w_lo = sb("w_lo", [P, W_TOTAL], F32R)
        late_tiles = sb("late_tiles", [P, 15, T])
        assert W_TOTAL <= 15 * T
        w_raw = late_tiles[:].rearrange("p i t -> p (i t)")[:, 0:W_TOTAL]
        (tanh_r, tanh_z, gh_n, r_gh, n_in, n_gate, h_minus_n, x1_plus_n, z_part, conv_sum,
         xc, out_sb) = (late_tiles[:, i] for i in range(12))
        exp_dist, kernel_a, msg = (late_tiles[:, i].rearrange("p (g n) -> p g n", g=PER) for i in range(12, 15))
        vec = sb("vec", [P, len(V_NAMES)])
        b_msg_sb = sb("b_msg_sb", [P, PER, P])
        eps_col = sb("eps_col", [P, 1])
        eye = sb("eye", [P, P])
        eps_eye = sb("eps_eye", [P, PER, P])
        ones = sb("ones", [P, P], F32R)
        mean_col = sb("mean_col", [P, 1])
        minus_half = sb("minus_half", [P, PER])
        hb_bias = sb("hb_bias", [P, HC])
        bn_scale = sb("bn_scale", [P, 2])
        bn2_minus = sb("bn2_minus", [P, 1])
        bn_root = sb("bn_root", [P, 2])
        bn_inv = sb("bn_inv", [P, 2])
        bn_ms = sb("bn_ms", [P, 2])
        bn_bias = sb("bn_bias", [P, 2])
        gate_sum = sb("gate_sum", [P, 2])
        gate_bias = sb("gate_bias", [P, 2])

        x_in = sb("x_in", [P, 2, PER, P])
        adj_in = sb("adj_in", [P, 2, PER, P])
        xT_in = sb("xT_in", [P, 2, T])
        mask_in = sb("mask_in", [P, 2, PER, P])
        stats1 = sb("stats1", [P, PER, 6])
        moments1 = sb("moments1", [P, PER, 2])
        var1 = sb("var1", [P, PER])
        rstd1 = sb("rstd1", [P, PER])
        shift1 = sb("shift1", [P, PER])
        h1 = sb("h1", [P, PER, P])
        adj_eps = sb("adj_eps", [P, PER, P])
        agg_hi = sb("agg_hi", [P, T], F32R)
        agg_lo = sb("agg_lo", [P, T], F32R)
        sq = sb("sq", [P, HC, T])
        hb = sb("hb", [P, 2, HC, T])
        ms_eps = sb("ms_eps", [P, PER])
        rms = sb("rms", [P, PER])
        rms_hi = sb("rms_hi", [P, PER], F32R)
        rms_lo = sb("rms_lo", [P, PER], F32R)
        diag_hi = sb("diag_hi", [P, PER, P], F32R)
        diag_lo = sb("diag_lo", [P, PER, P], F32R)
        v = sb("v", [P, 2, T])
        tanh_v = sb("tanh_v", [P, 2, T])
        silu = sb("silu", [P, 2, T])
        silu_hi = sb("silu_hi", [P, HC, T], F32R)
        silu_lo = sb("silu_lo", [P, HC, T], F32R)
        x1 = sb("x1", [P, 2, T])
        stats2 = sb("stats2", [P, PER, 6])
        moments2 = sb("moments2", [P, PER, 2])
        var2 = sb("var2", [P, PER])
        rstd2 = sb("rstd2", [P, PER])
        shift2 = sb("shift2", [P, PER])
        h2_nodes = sb("h2_nodes", [P, PER, P])
        h2 = sb("h2", [P, 2, T])
        h2_hi = sb("h2_hi", [P, T], F32R)
        h2_lo = sb("h2_lo", [P, T], F32R)
        c1 = sb("c1", [P, 3, PER, PH])
        c1_hi = sb("c1_hi", [P, 3, PER, PADDED], F32R)
        c1_lo = sb("c1_lo", [P, 3, PER, PADDED], F32R)
        p1 = sb("p1", [P, PER, P1_COLS])
        mix_even = sb("mix_even", [P, PER, PH])
        mix_odd = sb("mix_odd", [P, PER, PH])
        even_part = sb("even_part", [P, PER * PH])
        dist_l = sb("dist_l", [96, T])
        dist_r = sb("dist_r", [96, T])
        nmp_hi = sb("nmp_hi", [P, T], F32R)
        nmp_lo = sb("nmp_lo", [P, T], F32R)
        xc_hi = sb("xc_hi", [P, T], F32R)
        xc_lo = sb("xc_lo", [P, T], F32R)

        bank = [ctx.enter_context(nc.psum_tensor(f"bank{i}", [P, T], F32)) for i in range(8)]
        conv2_p0, conv2_p2 = bank[0][:, 0:PER * PH], bank[0][:, PER * PH:T]
        conv2_p1 = bank[2][:, 0:PER * P1_COLS]
        conv1_ps = agg_ps = dist_ps = x1_nodes_ps = bank[1]
        seed_ps = w2_ps = ms_ps = bank[2]
        msg_ps = nmp_ps = h2_ps = bank[3]
        rms_ps = r_ps = bank[4]
        z_ps, hn_ps, in_ps = bank[5], bank[6], bank[7]
        w1_ps = [bank[3], bank[5], bank[6], bank[7]]

        raw_loaded = [sem(f"raw_loaded{i}") for i in range(3)]
        small_loaded = sem("small_loaded")
        split_hi, split_lo_first, split_lo_rest = sem("split_hi"), sem("split_lo_first"), sem("split_lo_rest")
        const_ready, eye_zeroed, eye_ready = sem("const_ready"), sem("eye_zeroed"), sem("eye_ready")
        prep, root_ready = sem("prep"), sem("root_ready")
        x_loaded = [sem(f"x_loaded{i}") for i in range(2)]
        adj_loaded = [sem(f"adj_loaded{i}") for i in range(2)]
        xT_loaded = [sem(f"xT_loaded{i}") for i in range(2)]
        mask_loaded = [sem(f"mask_loaded{i}") for i in range(2)]
        stats1_ready, moments1_ready, var1_ready = sem("stats1_ready"), sem("moments1_ready"), sem("var1_ready")
        rstd1_ready, shift1_ready = sem("rstd1_ready"), sem("shift1_ready")
        h1_ready, adj_eps_ready = sem("h1_ready"), sem("adj_eps_ready")
        agg_done, agg_hi_ready, agg_lo_ready = sem("agg_done"), sem("agg_hi_ready"), sem("agg_lo_ready")
        w1_done = [sem(f"w1_done{c}") for c in range(HC)]
        sq_ready = [sem(f"sq_ready{c}") for c in range(HC)]
        hb_ready = [sem(f"hb_ready{c}") for c in range(HC)]
        sq_pairs, sq_sum_ready = sem("sq_pairs"), sem("sq_sum_ready")
        ms_done, ms_eps_ready, rms_ready = sem("ms_done"), sem("ms_eps_ready"), sem("rms_ready")
        rms_hi_ready, rms_lo_ready = sem("rms_hi_ready"), sem("rms_lo_ready")
        diag_ready, rms_done = sem("diag_ready"), sem("rms_done")
        v_ready = [sem(f"v_ready{c}") for c in range(HC)]
        tanh_ready = [sem(f"tanh_ready{c}") for c in range(HC)]
        silu_ready = [sem(f"silu_ready{c}") for c in range(HC)]
        silu_hi_ready = [sem(f"silu_hi_ready{c}") for c in range(HC)]
        silu_lo_ready = [sem(f"silu_lo_ready{c}") for c in range(HC)]
        w2_done, x1_ready, x1_nodes_done = sem("w2_done"), sem("x1_ready"), sem("x1_nodes_done")
        stats2_ready, moments2_ready, var2_ready = sem("stats2_ready"), sem("moments2_ready"), sem("var2_ready")
        rstd2_ready, shift2_ready, h2_nodes_ready = sem("rstd2_ready"), sem("shift2_ready"), sem("h2_nodes_ready")
        pairs_ready = sem("pairs_ready")
        h2_done, h2_ready, h2_hi_ready, h2_lo_ready = sem("h2_done"), sem("h2_ready"), sem("h2_hi_ready"), sem("h2_lo_ready")
        conv1_done, c1_ready, c1_hi_ready, c1_lo_ready = sem("conv1_done"), sem("c1_ready"), sem("c1_hi_ready"), sem("c1_lo_ready")
        seed_done, dist_ops_ready, dist_done, a_ready = sem("seed_done"), sem("dist_ops_ready"), sem("dist_done"), sem("a_ready")
        exp_ready = sem("exp_ready")
        msg_done, msg_sum_ready, msg_ready = sem("msg_done"), sem("msg_sum_ready"), sem("msg_ready")
        nmp_done, nmp_hi_ready, nmp_lo_ready = sem("nmp_done"), sem("nmp_hi_ready"), sem("nmp_lo_ready")
        c1_sum_ready, c1_sum_hi_ready, c1_sum_lo_ready = sem("c1_sum_ready"), sem("c1_sum_hi_ready"), sem("c1_sum_lo_ready")
        p1_done, p1_ready, mix_ready, even_part_ready = sem("p1_done"), sem("p1_ready"), sem("mix_ready"), sem("even_part_ready")
        conv2_done, conv_sum_ready, xc_ready = sem("conv2_done"), sem("conv_sum_ready"), sem("xc_ready")
        xc_hi_ready, xc_lo_ready = sem("xc_hi_ready"), sem("xc_lo_ready")
        r_done, z_done, hn_done, in_done = sem("r_done"), sem("z_done"), sem("hn_done"), sem("in_done")
        tanh_r_ready, tanh_z_ready, gh_n_ready = sem("tanh_r_ready"), sem("tanh_z_ready"), sem("gh_n_ready")
        r_gh_ready, n_in_ready, n_ready = sem("r_gh_ready"), sem("n_in_ready"), sem("n_ready")
        h_minus_n_ready, x1_plus_n_ready = sem("h_minus_n_ready"), sem("x1_plus_n_ready")
        z_part_ready, out_ready, stored = sem("z_part_ready"), sem("out_ready"), sem("stored")

        def need(eng, semaphore, groups):
            if type(groups) is int:
                if groups <= 0:
                    return
                groups = min(groups, NG)
            eng.wait_ge(semaphore, groups)

        def need_load(eng, semaphores, g, parity):
            eng.wait_ge(semaphores[parity], g * 8 + (16 - 8 * parity))

        def steps(eng, step, first=-3, last=NG):
            for t in range(first, LOOP_FIRST):
                step(t, t % 2)
            with eng.Fori(LOOP_FIRST, LOOP_END, 2) as t:
                for k in range(2):
                    step(t + k if k else t, (LOOP_FIRST + k) % 2)
            for t in range(LOOP_END, last + 1):
                step(t, t % 2)

        def has(t, lag):
            return type(t) is not int or 0 <= t + lag < NG

        def w(part, name, block):
            at = W_AT[name] + block * P
            return part[:, at:at + P]

        def bias(name):
            return vec[:, V_AT[name]:V_AT[name] + 1]

        def cols(name, n):
            return vec[:, V_AT[name]:V_AT[name] + n]

        def graph(j):
            return slice(j * P, (j + 1) * P)

        LOTS = [slice(0, W_AT["ih"]), slice(W_AT["ih"], W_AT["conv2"]), slice(W_AT["conv2"], W_TOTAL)]

        block = ctx.enter_context(nc.Block())

        @block.sync
        def _(sp):
            def load_x(g, parity):
                need(sp, h1_ready, g - 1)
                sp.dma_start(x_in[:, parity], x_nodes[g]).then_inc(x_loaded[parity], 16)
                need(sp, adj_eps_ready, g - 1)
                sp.dma_start(adj_in[:, parity], adj_t[g]).then_inc(adj_loaded[parity], 16)

            def load_xT(g, parity):
                need(sp, x1_ready, g - 1)
                sp.dma_start(xT_in[:, parity], x_feats[g]).then_inc(xT_loaded[parity], 16)

            def load_mask(g, parity):
                need(sp, a_ready, g - 1)
                sp.dma_start(mask_in[:, parity], adj_t[g]).then_inc(mask_loaded[parity], 16)

            def store(g):
                need(sp, out_ready, g + 1)
                sp.dma_start(out[g], out_sb).then_inc(stored, 16)

            def load_weights(lot):
                at = slice(LOTS[lot].start, min(LOTS[lot].stop, weights.shape[1]))
                sp.dma_start(w_raw[:, at], weights[:, at]).then_inc(raw_loaded[lot], 16)

            sp.dma_start(vec[:], vectors).then_inc(small_loaded, 16)
            sp.dma_start(eps_col[:], epsilon.partition_broadcast(P)).then_inc(small_loaded, 16)
            sp.dma_start(b_msg_sb[:], b_msg.partition_broadcast(P)).then_inc(small_loaded, 16)
            load_x(0, 0)
            load_weights(0)
            load_weights(2)
            load_weights(1)
            load_x(1, 1)
            load_xT(0, 0)
            load_xT(1, 1)

            def step(t, parity):
                if has(t, 4) and not (type(t) is int and t + 4 < 2):
                    load_x(t + 4, parity)
                if has(t, 2) and not (type(t) is int and t + 2 < 2):
                    load_xT(t + 2, parity)
                if has(t, 1):
                    load_mask(t + 1, 1 - parity)
                if has(t, -1):
                    store(t - 1)

            for t in range(-2, 1):
                step(t, t % 2)
            with sp.Fori(1, 11, 2) as t:
                for k in range(2):
                    step(t + k if k else t, (1 + k) % 2)
            for t in range(11, NG + 1):
                step(t, t % 2)
            sp.wait_ge(stored, 16 * NG)

        @block.tensor
        def _(pe):
            def exact(out_ps, name, block_, hi, lo, first, last):
                with_high(out_ps, name, block_, hi, first)
                return with_low(out_ps, name, block_, lo, last)

            def with_high(out_ps, name, block_, hi, first):
                nc.tensor.matmul(out_ps, w(w_hi, name, block_), hi, start=first, stop=False)
                nc.tensor.matmul(out_ps, w(w_lo, name, block_), hi, start=False, stop=False)

            def with_low(out_ps, name, block_, lo, last):
                return nc.tensor.matmul(out_ps, w(w_hi, name, block_), lo, start=False, stop=last)

            def conv1(g):
                need(pe, h2_hi_ready, g + 1)
                with_high(conv1_ps[:], "conv1", 0, h2_hi[:], True)
                need(pe, h2_lo_ready, g + 1)
                with_low(conv1_ps[:], "conv1", 0, h2_lo[:], True).then_inc(conv1_done, 1)

            def seeds(g):
                need(pe, ms_eps_ready, g + 2)
                exact(seed_ps[:], "se", 0, h2_hi[:], h2_lo[:], True, True).then_inc(seed_done, 1)

            def messages(g):
                for j in range(PER):
                    ps = msg_ps[:, graph(j)]
                    nc.tensor.matmul(ps, h2_hi[:, graph(j)], w(w_hi, "msg", 0), start=True, stop=False)
                    nc.tensor.matmul(ps, h2_hi[:, graph(j)], w(w_lo, "msg", 0), start=False, stop=False)
                    last = nc.tensor.matmul(ps, h2_lo[:, graph(j)], w(w_hi, "msg", 0), start=False, stop=True)
                last.then_inc(msg_done, 1)

            def aggregate(g):
                need(pe, h1_ready, g + 1)
                need(pe, adj_eps_ready, g + 1)
                need(pe, c1_ready, g - 1)
                for j in range(PER):
                    last = nc.tensor.matmul(agg_ps[:, graph(j)], h1[:, j], adj_eps[:, j], start=True, stop=True)
                last.then_inc(agg_done, 1)

            def rms_rows(g):
                need(pe, diag_ready, g + 1)
                need(pe, tanh_r_ready, g - 1)
                nc.tensor.matmul(rms_ps[:], ones[:], diag_hi[:].rearrange("p g n -> p (g n)"), start=True, stop=False)
                nc.tensor.matmul(rms_ps[:], ones[:], diag_lo[:].rearrange("p g n -> p (g n)"), start=False,
                                 stop=True).then_inc(rms_done, 1)

            def w1(g):
                need(pe, agg_hi_ready, g + 1)
                need(pe, agg_lo_ready, g + 1)
                for c, (semaphore, groups) in enumerate(((msg_sum_ready, g - 1), (tanh_z_ready, g - 2),
                                                         (gh_n_ready, g - 2), (n_in_ready, g - 2))):
                    need(pe, semaphore, groups)
                    exact(w1_ps[c][:], "w1", c, agg_hi[:], agg_lo[:], True, True).then_inc(w1_done[c], 1)

            def distances(g):
                need(pe, dist_ops_ready, g + 1)
                need(pe, agg_hi_ready, g + 3)
                need(pe, agg_lo_ready, g + 3)
                for j in range(PER):
                    last = nc.tensor.matmul(dist_ps[:, graph(j)], dist_l[:, graph(j)], dist_r[:, graph(j)],
                                            start=True, stop=True)
                last.then_inc(dist_done, 1)

            def half_conv(out_ps, width, phase, tap_blocks, parts):
                n_taps = len(tap_blocks)
                order = sorted(range(n_taps), key=lambda k: abs(k - HALF // 2))
                for k in order[parts]:
                    s = k - HALF // 2
                    a = max(0, -s) & ~1
                    b = width if k == order[0] else min(width, (PH - s + 1) & ~1)
                    hi, lo = (c[:, phase, :, a + s + 1:b + s + 1] for c in (c1_hi, c1_lo))
                    last = exact(out_ps[:, :, a:b], *tap_blocks[k], hi, lo, k == order[0], k == order[-1])
                return last

            even_taps = [("conv2", 2 * a) for a in range(HALF + 1)]
            odd_taps = [("conv2", 2 * a + 1) for a in range(HALF)]
            pair_taps = [("conv2_pairs", a) for a in range(HALF)] + [("conv2", TAPS - 1)]

            def conv2_p1_product(g):
                need(pe, c1_hi_ready, g + 1)
                need(pe, c1_lo_ready, g + 1)
                need(pe, dist_ops_ready, g + 1)
                half_conv(conv2_p1.rearrange("p (g n) -> p g n", g=PER), P1_COLS, 0, odd_taps,
                          slice(None)).then_inc(p1_done, 1)

            def conv2_p0_product(g):
                need(pe, conv_sum_ready, g)
                half_conv(conv2_p0.rearrange("p (g n) -> p g n", g=PER), PH, 1, even_taps, slice(None))

            def conv2_p2_product(g, parts):
                need(pe, c1_sum_hi_ready, g + 1)
                need(pe, c1_sum_lo_ready, g + 1)
                return half_conv(conv2_p2.rearrange("p (g n) -> p g n", g=PER), PH, 2, pair_taps, parts)

            def w2(g, c):
                if c == 0:
                    need(pe, p1_ready, g)
                need(pe, silu_hi_ready[c], g + 1)
                need(pe, silu_lo_ready[c], g + 1)
                last = exact(w2_ps[:], "w2", c, silu_hi[:, c], silu_lo[:, c], c == 0, c == HC - 1)
                if c == HC - 1:
                    last.then_inc(w2_done, 1)

            def gather(g):
                need(pe, a_ready, g + 1)
                need(pe, msg_ready, g + 1)
                need(pe, sq_ready[0], g + 3)
                need(pe, hb_ready[0], g + 3)
                for j in range(PER):
                    last = nc.tensor.matmul(nmp_ps[:, graph(j)], msg[:, j], kernel_a[:, j], start=True, stop=True)
                last.then_inc(nmp_done, 1)

            def x1_by_nodes(g, parity):
                need(pe, x1_ready, g + 1)
                need(pe, exp_ready, g)
                for j in range(PER):
                    last = nc.tensor.transpose(x1_nodes_ps[:, graph(j)], x1[:, parity, graph(j)], eye[:])
                last.then_inc(x1_nodes_done, 1)

            def mean_squares(g):
                need(pe, sq_sum_ready, g + 1)
                need(pe, x1_ready, g)
                for j in range(PER):
                    last = nc.tensor.matmul(ms_ps[:, j:j + 1], sq[:, 0, graph(j)], mean_col[:], start=True, stop=True)
                last.then_inc(ms_done, 1)

            def h2_by_features(g):
                need(pe, h2_nodes_ready, g + 1)
                need(pe, nmp_hi_ready, g)
                need(pe, nmp_lo_ready, g)
                for j in range(PER):
                    last = nc.tensor.transpose(h2_ps[:, graph(j)], h2_nodes[:, j], eye[:])
                last.then_inc(h2_done, 1)

            def gates_early(g):
                need(pe, nmp_hi_ready, g + 1)
                need(pe, nmp_lo_ready, g + 1)
                need(pe, v_ready[HC - 1], g + 2)
                exact(r_ps[:], "hh", 0, h2_hi[:], h2_lo[:], True, False)
                exact(r_ps[:], "ih", 3, nmp_hi[:], nmp_lo[:], False, False)
                for c in range(1, HC):
                    need(pe, sq_ready[c], g + 3)
                    need(pe, hb_ready[c], g + 3)
                exact(z_ps[:], "hh", 1, h2_hi[:], h2_lo[:], True, False)
                exact(z_ps[:], "ih", 4, nmp_hi[:], nmp_lo[:], False, False)
                exact(hn_ps[:], "hh", 2, h2_hi[:], h2_lo[:], True, True).then_inc(hn_done, 1)
                exact(in_ps[:], "ih", 5, nmp_hi[:], nmp_lo[:], True, False)

            def gates_late(g):
                need(pe, xc_hi_ready, g + 1)
                with_high(r_ps[:], "ih", 0, xc_hi[:], False)
                need(pe, xc_lo_ready, g + 1)
                with_low(r_ps[:], "ih", 0, xc_lo[:], True).then_inc(r_done, 1)
                exact(z_ps[:], "ih", 1, xc_hi[:], xc_lo[:], False, True).then_inc(z_done, 1)
                exact(in_ps[:], "ih", 2, xc_hi[:], xc_lo[:], False, True).then_inc(in_done, 1)

            def step(t, parity):
                if has(t, 0):
                    if type(t) is int and t == 0:
                        pe.wait_ge(split_hi, 3)
                        pe.wait_ge(split_lo_rest, 2)
                    conv1(t)
                    seeds(t)
                    messages(t)
                if has(t, 2):
                    if type(t) is int and t == -2:
                        pe.wait_ge(eye_ready, 1)
                        pe.wait_ge(const_ready, 1)
                    aggregate(t + 2)
                    if type(t) is int and t == -2:
                        pe.wait_ge(split_hi, 1)
                        pe.wait_ge(split_lo_first, 1)
                        pe.wait_ge(small_loaded, 48)
                if has(t, 1):
                    rms_rows(t + 1)
                if has(t, 0):
                    conv2_p1_product(t)
                    distances(t)
                if has(t, 2):
                    w1(t + 2)
                if has(t, 0):
                    conv2_p0_product(t)
                if has(t, 1):
                    w2(t + 1, 0)
                    w2(t + 1, 1)
                if has(t, 0):
                    gather(t)
                if has(t, 1):
                    w2(t + 1, 2)
                    w2(t + 1, 3)
                if has(t, 0):
                    conv2_p2_product(t, slice(0, 6))
                if has(t, 1):
                    x1_by_nodes(t + 1, 1 - parity)
                if has(t, 0):
                    conv2_p2_product(t, slice(6, None)).then_inc(conv2_done, 1)
                if has(t, 0):
                    gates_early(t)
                if has(t, 2):
                    mean_squares(t + 2)
                if has(t, 1):
                    h2_by_features(t + 1)
                if has(t, 0):
                    gates_late(t)

            steps(pe, step)

        @block.scalar
        def _(act):
            act.wait_ge(prep, 1)
            nc.scalar.activation(bn_root[:], bn_root[:], ACT.Sqrt).then_inc(root_ready, 1)

            def split_high(lot):
                act.wait_ge(raw_loaded[lot], 16)
                if lot == 2:
                    act.wait_ge(pairs_ready, 1)
                nc.scalar.copy(w_hi[:, LOTS[lot]], w_raw[:, LOTS[lot]]).then_inc(split_hi, 1)

            for lot in range(3):
                split_high(lot)
            act.wait_ge(prep, 10)

            def r_and_z(g):
                need(act, r_done, g + 1)
                need(act, r_gh_ready, g)
                nc.scalar.activation(tanh_r, r_ps[:], ACT.Tanh, bias=gate_bias[:, 0:1], scale=0.5).then_inc(tanh_r_ready, 1)
                need(act, hn_done, g + 1)
                nc.scalar.activation(gh_n, hn_ps[:], ACT.Identity, bias=bias("bhh_n")).then_inc(gh_n_ready, 1)
                need(act, z_done, g + 1)
                need(act, z_part_ready, g)
                nc.scalar.activation(tanh_z, z_ps[:], ACT.Tanh, bias=gate_bias[:, 1:2], scale=0.5).then_inc(tanh_z_ready, 1)

            def n_of(g):
                need(act, n_in_ready, g + 1)
                need(act, h_minus_n_ready, g)
                need(act, x1_plus_n_ready, g)
                nc.scalar.activation(n_gate, n_in, ACT.Tanh, bias=bias("bih_n")).then_inc(n_ready, 1)

            def conv1_relu(g):
                need(act, conv1_done, g + 1)
                need(act, c1_lo_ready, g)
                need(act, c1_sum_ready, g)
                nc.scalar.activation(c1[:, 0:2].rearrange("p ph g i -> p g i ph"),
                                     conv1_ps[:].rearrange("p (g i ph) -> p g i ph", g=PER, ph=2), ACT.Relu,
                                     bias=bn_bias[:, 0:1], scale=bn_scale[:, 0:1]).then_inc(c1_ready, 1)

            def distance_operands(g):
                need(act, seed_done, g + 1)
                need(act, dist_done, g)
                nc.scalar.activation(dist_l[0:32], seed_ps[0:32], ACT.Identity, bias=bias("bse")[0:32])
                nc.scalar.activation(dist_r[0:32], seed_ps[0:32], ACT.Identity, bias=bias("bse")[0:32])
                nc.scalar.activation(dist_l[32:64], seed_ps[32:64], ACT.Square, bias=bias("bse")[32:64])
                nc.scalar.activation(dist_r[64:96], seed_ps[64:96], ACT.Square, bias=bias("bse")[64:96]).then_inc(dist_ops_ready, 1)

            def aggregate_high(g):
                need(act, agg_done, g + 1)
                need(act, w1_done[HC - 1], g)
                nc.scalar.copy(agg_hi[:], agg_ps[:]).then_inc(agg_hi_ready, 1)

            def p1_scaled(g):
                need(act, p1_done, g + 1)
                need(act, mix_ready, g)
                nc.scalar.activation(p1[:].rearrange("p g n -> p (g n)"), conv2_p1, ACT.Identity,
                                     scale=bn_scale[:, 1:2]).then_inc(p1_ready, 1)

            def silu_tanh(g, chunks):
                for c in chunks:
                    need(act, v_ready[c], g + 1)
                    need(act, silu_ready[(c + 2) % HC], g + (1 if c >= 2 else 0))
                    nc.scalar.activation(tanh_v[:, c % 2], v[:, c % 2], ACT.Tanh).then_inc(tanh_ready[c], 1)

            def hidden(g, parity):
                for c in range(HC):
                    need(act, w1_done[c], g + 1)
                    if c == 0:
                        need(act, ms_done, g)
                        need(act, v_ready[HC - 1], g - 1)
                    nc.scalar.activation(sq[:, c], w1_ps[c][:], ACT.Square, bias=bias(f"b1_{c}")).then_inc(sq_ready[c], 1)
                    nc.scalar.activation(hb[:, parity, c], w1_ps[c][:], ACT.Identity, bias=hb_bias[:, c:c + 1],
                                         scale=bias(f"rms_{c}")).then_inc(hb_ready[c], 1)

            def exponential(g):
                need(act, dist_done, g + 1)
                need(act, a_ready, g)
                nc.scalar.activation(exp_dist.rearrange("p g n -> p (g n)"), dist_ps[:], ACT.Exp, scale=2.0).then_inc(exp_ready, 1)

            def layernorm1_relu(g, parity):
                need(act, shift1_ready, g + 1)
                need(act, agg_done, g)
                for j in range(PER):
                    last = nc.scalar.activation(h1[:, j], x_in[:, parity, j], ACT.Relu, bias=shift1[:, j:j + 1],
                                                scale=rstd1[:, j:j + 1])
                last.then_inc(h1_ready, 1)

            def gathered_high(g):
                need(act, nmp_done, g + 1)
                need(act, in_done, g)
                nc.scalar.copy(nmp_hi[:], nmp_ps[:]).then_inc(nmp_hi_ready, 1)

            def layernorm2_relu(g):
                need(act, shift2_ready, g + 1)
                need(act, h2_done, g)
                for j in range(PER):
                    last = nc.scalar.activation(h2_nodes[:, j], x1_nodes_ps[:, graph(j)], ACT.Relu,
                                                bias=shift2[:, j:j + 1], scale=rstd2[:, j:j + 1])
                last.then_inc(h2_nodes_ready, 1)

            def conv2_high(g):
                need(act, conv_sum_ready, g + 1)
                need(act, in_done, g)
                nc.scalar.activation(xc_hi[:], conv_sum, ACT.Relu, bias=bn_bias[:, 1:2]).then_inc(xc_hi_ready, 1)

            def h2_full(g, parity):
                need(act, h2_done, g + 1)
                need(act, hn_done, g)
                nc.scalar.copy(h2_hi[:], h2_ps[:]).then_inc(h2_hi_ready, 1)
                need(act, h_minus_n_ready, g - 1)
                nc.scalar.copy(h2[:, parity], h2_ps[:]).then_inc(h2_ready, 1)

            def step(t, parity):
                if has(t, -1):
                    r_and_z(t - 1)
                if has(t, 0):
                    conv1_relu(t)
                    distance_operands(t)
                if has(t, -1):
                    n_of(t - 1)
                if has(t, 2):
                    aggregate_high(t + 2)
                if has(t, 1):
                    silu_tanh(t + 1, (0, 1))
                if has(t, 0):
                    p1_scaled(t)
                if has(t, 1):
                    silu_tanh(t + 1, (2,))
                if has(t, 0):
                    exponential(t)
                if has(t, 1):
                    silu_tanh(t + 1, (3,))
                if has(t, 2):
                    hidden(t + 2, parity)
                if has(t, 0):
                    gathered_high(t)
                if has(t, 3):
                    layernorm1_relu(t + 3, 1 - parity)
                if has(t, 1):
                    layernorm2_relu(t + 1)
                if has(t, 0):
                    conv2_high(t)
                if has(t, 1):
                    h2_full(t + 1, 1 - parity)

            steps(act, step)

        @block.vector
        def _(dve):
            done = [0]

            def chained(ins):
                done[0] += 1
                ins.then_inc(prep, 1)
                dve.wait_ge(prep, done[0])

            for phase in range(3):
                for c in (c1_hi, c1_lo):
                    nc.vector.memset(c[:, phase, :, 0:1].bitcast(F32), 0.0)
                    nc.vector.memset(c[:, phase, :, PH + 1:PADDED].bitcast(F32), 0.0)
            nc.vector.memset(dist_l[64:96], -0.5)
            nc.vector.memset(dist_r[32:64], -0.5)
            nc.vector.memset(mean_col[:], 1.0 / (HC * P))
            nc.vector.memset(minus_half[:], -0.5)
            nc.vector.memset(ones[:].bitcast(F32), 1.0).then_inc(const_ready, 1)
            dve.wait_ge(small_loaded, 48)
            chained(nc.vector.tensor_scalar(bn_root[:], cols("bn1_v", 2), BN_EPS, None, ALU.add))
            chained(nc.vector.tensor_scalar(cols("rms_0", HC), cols("rms_0", HC), 0.5, None, ALU.mult))
            chained(nc.vector.tensor_tensor(hb_bias[:], cols("b1_0", HC), cols("rms_0", HC), ALU.mult))
            chained(nc.vector.tensor_tensor(gate_sum[:], cols("bih_r", 2), cols("bhh_r", 2), ALU.add))
            chained(nc.vector.tensor_scalar(gate_bias[:], gate_sum[:], 0.5, None, ALU.mult))
            dve.wait_ge(root_ready, 1)
            chained(nc.vector.reciprocal(bn_inv[:], bn_root[:]))
            chained(nc.vector.tensor_tensor(bn_scale[:], bn_inv[:], cols("bn1_g", 2), ALU.mult))
            chained(nc.vector.tensor_tensor(bn_ms[:], bn_scale[:], cols("bn1_m", 2), ALU.mult))
            chained(nc.vector.tensor_tensor(bn_bias[:], cols("bn1_b", 2), bn_ms[:], ALU.subtract))
            chained(nc.vector.tensor_scalar(bn2_minus[:], bn_scale[:, 1:2], -1.0, None, ALU.mult))

            def split_low_first():
                dve.wait_ge(split_hi, 1)
                nc.vector.tensor_tensor(w_lo[:, LOTS[0]], w_raw[:, LOTS[0]], w_hi[:, LOTS[0]].bitcast(F32),
                                        ALU.subtract).then_inc(split_lo_first, 1)

            def reset_and_input(g):
                need(dve, tanh_r_ready, g + 1)
                need(dve, gh_n_ready, g + 1)
                need(dve, n_in_ready, g)
                nc.vector.scalar_tensor_tensor(r_gh, tanh_r, 1.0, gh_n, ALU.add, ALU.mult).then_inc(r_gh_ready, 1)
                need(dve, r_gh_ready, g + 1)
                need(dve, in_done, g + 1)
                need(dve, n_ready, g)
                nc.vector.scalar_tensor_tensor(n_in, r_gh, 0.5, in_ps[:], ALU.mult, ALU.add).then_inc(n_in_ready, 1)

            def interior(padded, a, b):
                return padded[:, a:b].rearrange("p ph g i -> p (ph g) i")[:, :, 1:PH + 1]

            def by_graph(phases, a, b):
                return phases[:, a:b].rearrange("p ph g i -> p (ph g) i")

            def conv1_split(g):
                need(dve, c1_ready, g + 1)
                need(dve, conv2_done, g)
                nc.vector.tensor_copy(interior(c1_hi, 0, 2), by_graph(c1, 0, 2)).then_inc(c1_hi_ready, 1)
                need(dve, c1_hi_ready, g + 1)
                nc.vector.tensor_tensor(interior(c1_lo, 0, 2), by_graph(c1, 0, 2), interior(c1_hi, 0, 2).bitcast(F32),
                                        ALU.subtract).then_inc(c1_lo_ready, 1)

            def conv1_sum_split(g):
                need(dve, c1_sum_lo_ready, g)
                nc.vector.tensor_tensor(c1[:, 2], c1[:, 0], c1[:, 1], ALU.add).then_inc(c1_sum_ready, 1)
                need(dve, c1_sum_ready, g + 1)
                nc.vector.tensor_copy(interior(c1_hi, 2, 3), by_graph(c1, 2, 3)).then_inc(c1_sum_hi_ready, 1)
                need(dve, c1_sum_hi_ready, g + 1)
                nc.vector.tensor_tensor(interior(c1_lo, 2, 3), by_graph(c1, 2, 3), interior(c1_hi, 2, 3).bitcast(F32),
                                        ALU.subtract).then_inc(c1_sum_lo_ready, 1)

            def message_relu(g):
                need(dve, msg_done, g + 1)
                need(dve, nmp_done, g)
                nc.vector.tensor_tensor(msg, msg_ps[:].rearrange("p (g n) -> p g n", n=P), b_msg_sb[:],
                                        ALU.add).then_inc(msg_sum_ready, 1)
                need(dve, msg_sum_ready, g + 1)
                nc.vector.tensor_scalar(msg, msg, 0.0, None, ALU.max).then_inc(msg_ready, 1)

            def aggregate_low(g):
                need(dve, agg_hi_ready, g + 1)
                nc.vector.tensor_tensor(agg_lo[:], agg_ps[:], agg_hi[:].bitcast(F32), ALU.subtract).then_inc(agg_lo_ready, 1)

            def v_of(g, parity, c):
                if c == 0:
                    need(dve, rms_done, g + 1)
                need(dve, hb_ready[c], g + 1)
                need(dve, silu_ready[(c + 2) % HC], g + (1 if c >= 2 else 0))
                nc.vector.tensor_tensor(v[:, c % 2], rms_ps[:], hb[:, parity, c], ALU.mult).then_inc(v_ready[c], 1)

            def masked(g, parity):
                need(dve, exp_ready, g + 1)
                need_load(dve, mask_loaded, g, parity)
                need(dve, nmp_done, g)
                nc.vector.tensor_tensor(kernel_a, exp_dist, mask_in[:, parity], ALU.mult).then_inc(a_ready, 1)

            def silu_of(g, c):
                need(dve, tanh_ready[c], g + 1)
                need(dve, silu_lo_ready[(c + 2) % HC], g + (1 if c >= 2 else 0))
                nc.vector.scalar_tensor_tensor(silu[:, c % 2], tanh_v[:, c % 2], 1.0, v[:, c % 2], ALU.add,
                                               ALU.mult).then_inc(silu_ready[c], 1)
                need(dve, silu_ready[c], g + 1)
                need(dve, w2_done, g)
                nc.vector.tensor_copy(silu_hi[:, c], silu[:, c % 2]).then_inc(silu_hi_ready[c], 1)

            def state(g):
                need(dve, h_minus_n_ready, g + 1)
                need(dve, tanh_z_ready, g + 1)
                need(dve, out_ready, g)
                nc.vector.scalar_tensor_tensor(z_part, tanh_z, 1.0, h_minus_n, ALU.add, ALU.mult).then_inc(z_part_ready, 1)
                need(dve, z_part_ready, g + 1)
                need(dve, x1_plus_n_ready, g + 1)
                dve.wait_ge(stored, g * 16) if type(g) is not int or g > 0 else None
                nc.vector.scalar_tensor_tensor(out_sb, z_part, 0.5, x1_plus_n, ALU.mult, ALU.add).then_inc(out_ready, 1)

            def layernorm1_stats(g, parity):
                need_load(dve, x_loaded, g, parity)
                for j in range(PER):
                    last = nc.vector.bn_stats(stats1[:, j], x_in[:, parity, j])
                last.then_inc(stats1_ready, 1)

            def layernorm1_moments(g):
                need(dve, rstd1_ready, g)
                need(dve, stats1_ready, g + 1)
                nc.vector.memset(var1[:], 0.0)
                for j in range(PER):
                    last = nc.vector.bn_aggr(moments1[:, j], stats1[:, j])
                last.then_inc(moments1_ready, 1)
                need(dve, moments1_ready, g + 1)
                nc.vector.tensor_scalar(var1[:], moments1[:, :, 1], LN_EPS, None, ALU.add).then_inc(var1_ready, 1)

            def layernorm1_shift(g):
                need(dve, rstd1_ready, g + 1)
                need(dve, h1_ready, g)
                nc.vector.scalar_tensor_tensor(shift1[:], moments1[:, :, 0], -1.0, rstd1[:], ALU.mult, ALU.mult).then_inc(shift1_ready, 1)

            def gathered_low(g):
                need(dve, nmp_hi_ready, g + 1)
                nc.vector.tensor_tensor(nmp_lo[:], nmp_ps[:], nmp_hi[:].bitcast(F32), ALU.subtract).then_inc(nmp_lo_ready, 1)

            def residual1(g, parity):
                need(dve, w2_done, g + 1)
                need_load(dve, xT_loaded, g, parity)
                need(dve, x1_plus_n_ready, g - 1)
                nc.vector.scalar_tensor_tensor(x1[:, parity], w2_ps[:], bias("b2"), xT_in[:, parity], ALU.add,
                                               ALU.add).then_inc(x1_ready, 1)

            def mean_square_eps(g):
                need(dve, ms_done, g + 1)
                need(dve, rms_ready, g)
                nc.vector.tensor_scalar(ms_eps[:], ms_ps[:, 0:PER], RMS_EPS, None, ALU.add).then_inc(ms_eps_ready, 1)

            def layernorm2_stats(g):
                need(dve, x1_nodes_done, g + 1)
                for j in range(PER):
                    last = nc.vector.bn_stats(stats2[:, j], x1_nodes_ps[:, graph(j)])
                last.then_inc(stats2_ready, 1)

            def layernorm2_moments(g):
                need(dve, rstd2_ready, g)
                need(dve, stats2_ready, g + 1)
                nc.vector.memset(var2[:], 0.0)
                for j in range(PER):
                    last = nc.vector.bn_aggr(moments2[:, j], stats2[:, j])
                last.then_inc(moments2_ready, 1)
                need(dve, moments2_ready, g + 1)
                nc.vector.tensor_scalar(var2[:], moments2[:, :, 1], LN_EPS, None, ALU.add).then_inc(var2_ready, 1)

            def layernorm2_shift(g):
                need(dve, rstd2_ready, g + 1)
                need(dve, h2_nodes_ready, g)
                nc.vector.scalar_tensor_tensor(shift2[:], moments2[:, :, 0], -1.0, rstd2[:], ALU.mult, ALU.mult).then_inc(shift2_ready, 1)

            def rms_diagonals(g):
                need(dve, rms_ready, g + 1)
                need(dve, diag_ready, g)
                nc.vector.tensor_copy(rms_hi[:], rms[:]).then_inc(rms_hi_ready, 1)
                need(dve, rms_hi_ready, g + 1)
                nc.vector.tensor_tensor(rms_lo[:], rms[:], rms_hi[:].bitcast(F32), ALU.subtract).then_inc(rms_lo_ready, 1)
                need(dve, rms_done, g)
                for j in range(PER):
                    nc.vector.tensor_scalar(diag_hi[:, j], eye[:], rms_hi[:, j:j + 1].bitcast(F32), None, ALU.mult)
                need(dve, rms_lo_ready, g + 1)
                for j in range(PER):
                    last = nc.vector.tensor_scalar(diag_lo[:, j], eye[:], rms_lo[:, j:j + 1].bitcast(F32), None, ALU.mult)
                last.then_inc(diag_ready, 1)

            def conv2_relu(g):
                need(dve, conv2_done, g + 1)
                need(dve, mix_ready, g + 1)
                need(dve, xc_ready, g)
                nc.vector.scalar_tensor_tensor(even_part[:], conv2_p2, bn_scale[:, 1:2],
                                               mix_even[:].rearrange("p g i -> p (g i)"), ALU.mult,
                                               ALU.add).then_inc(even_part_ready, 1)
                nc.vector.scalar_tensor_tensor(conv_sum[:, 1:T:2], conv2_p0, bn_scale[:, 1:2],
                                               mix_odd[:].rearrange("p g i -> p (g i)"), ALU.mult, ALU.add)
                need(dve, even_part_ready, g + 1)
                nc.vector.scalar_tensor_tensor(conv_sum[:, 0:T:2], conv2_p0, bn2_minus[:], even_part[:], ALU.mult,
                                               ALU.add).then_inc(conv_sum_ready, 1)
                need(dve, conv_sum_ready, g + 1)
                need(dve, xc_lo_ready, g)
                nc.vector.tensor_scalar(xc, conv_sum, bn_bias[:, 1:2], 0.0, ALU.add, ALU.max).then_inc(xc_ready, 1)

            def conv2_low(g):
                need(dve, xc_ready, g + 1)
                need(dve, xc_hi_ready, g + 1)
                nc.vector.tensor_tensor(xc_lo[:], xc, xc_hi[:].bitcast(F32), ALU.subtract).then_inc(xc_lo_ready, 1)

            def h2_low(g, parity):
                need(dve, h2_ready, g + 1)
                need(dve, hn_done, g)
                nc.vector.tensor_tensor(h2_lo[:], h2[:, parity], h2_hi[:].bitcast(F32), ALU.subtract).then_inc(h2_lo_ready, 1)

            def step(t, parity):
                if type(t) is int and t == -2:
                    split_low_first()
                    dve.wait_ge(eye_ready, 1)
                if has(t, -1):
                    reset_and_input(t - 1)
                if has(t, 0):
                    conv1_split(t)
                    message_relu(t)
                if has(t, 2):
                    aggregate_low(t + 2)
                if has(t, 0):
                    conv1_sum_split(t)
                if has(t, 1):
                    v_of(t + 1, 1 - parity, 0)
                    v_of(t + 1, 1 - parity, 1)
                    silu_of(t + 1, 0)
                    v_of(t + 1, 1 - parity, 2)
                    silu_of(t + 1, 1)
                    v_of(t + 1, 1 - parity, 3)
                    silu_of(t + 1, 2)
                    silu_of(t + 1, 3)
                if has(t, 0):
                    masked(t, parity)
                if has(t, 3):
                    layernorm1_stats(t + 3, 1 - parity)
                    layernorm1_moments(t + 3)
                if has(t, -1):
                    state(t - 1)
                if has(t, 1):
                    residual1(t + 1, 1 - parity)
                if has(t, 0):
                    gathered_low(t)
                if has(t, 3):
                    layernorm1_shift(t + 3)
                if has(t, 1):
                    layernorm2_stats(t + 1)
                    layernorm2_moments(t + 1)
                if has(t, 1):
                    layernorm2_shift(t + 1)
                if has(t, 0):
                    conv2_relu(t)
                if has(t, 2):
                    mean_square_eps(t + 2)
                if has(t, 0):
                    conv2_low(t)
                if has(t, 1):
                    h2_low(t + 1, 1 - parity)
                if has(t, 2):
                    rms_diagonals(t + 2)

            steps(dve, step)

        @block.gpsimd
        def _(pool):
            nc.gpsimd.memset(eye[:], 0.0).then_inc(eye_zeroed, 1)
            pool.wait_ge(eye_zeroed, 1)
            nc.gpsimd.affine_select(out=eye[:], in_=eye[:], compare_op=ALU.not_equal, fill=1.0, base=0,
                                    pattern=[[-1, P]], channel_multiplier=1).then_inc(eye_ready, 1)
            pool.wait_ge(eye_ready, 1)
            pool.wait_ge(small_loaded, 48)
            for j in range(PER):
                last = nc.gpsimd.tensor_scalar(eps_eye[:, j], eye[:], eps_col[:, 0:1], None, ALU.mult)
            last.then_inc(eye_zeroed, 1)
            pool.wait_ge(eye_zeroed, 2)
            pool.wait_ge(const_ready, 1)

            def pair_weights():
                pool.wait_ge(raw_loaded[2], 16)
                taps = w_raw[:, W_AT["conv2"]:W_AT["conv2"] + 2 * HALF * P].rearrange("p (a two n) -> p a two n", two=2, n=P)
                pairs = w_raw[:, W_AT["conv2_pairs"]:W_TOTAL].rearrange("p (a n) -> p a n", n=P)
                nc.gpsimd.tensor_tensor(pairs, taps[:, :, 0], taps[:, :, 1], ALU.add).then_inc(pairs_ready, 1)

            def split_low(lot):
                pool.wait_ge(split_hi, lot + 1)
                nc.gpsimd.tensor_tensor(w_lo[:, LOTS[lot]], w_raw[:, LOTS[lot]], w_hi[:, LOTS[lot]].bitcast(F32),
                                        ALU.subtract).then_inc(split_lo_rest, 1)

            def blend_inputs(g, parity):
                need(pool, n_ready, g + 1)
                need(pool, z_part_ready, g)
                nc.gpsimd.tensor_tensor(h_minus_n, h2[:, parity], n_gate, ALU.subtract).then_inc(h_minus_n_ready, 1)
                need(pool, out_ready, g)
                nc.gpsimd.tensor_tensor(x1_plus_n, x1[:, parity], n_gate, ALU.add).then_inc(x1_plus_n_ready, 1)

            def conv2_mix(g, parity):
                need(pool, p1_ready, g + 1)
                need(pool, conv_sum_ready, g)
                h = h2[:, parity].rearrange("p (g i ph) -> p g i ph", g=PER, ph=2)
                nc.gpsimd.tensor_tensor(mix_even[:], h[:, :, :, 0], p1[:, :, 0:PH], ALU.subtract)
                nc.gpsimd.tensor_tensor(mix_odd[:], h[:, :, :, 1], p1[:, :, 1:PH + 1], ALU.add).then_inc(mix_ready, 1)

            def silu_low(g):
                for c in range(HC):
                    need(pool, silu_hi_ready[c], g + 1)
                    nc.gpsimd.tensor_tensor(silu_lo[:, c], silu[:, c % 2], silu_hi[:, c].bitcast(F32),
                                            ALU.subtract).then_inc(silu_lo_ready[c], 1)

            def square_sum(g):
                need(pool, sq_ready[1], g + 1)
                nc.gpsimd.tensor_tensor(sq[:, 0], sq[:, 0], sq[:, 1], ALU.add)
                need(pool, sq_ready[3], g + 1)
                nc.gpsimd.tensor_tensor(sq[:, 2], sq[:, 2], sq[:, 3], ALU.add).then_inc(sq_pairs, 1)
                need(pool, sq_pairs, g + 1)
                nc.gpsimd.tensor_tensor(sq[:, 0], sq[:, 0], sq[:, 2], ALU.add).then_inc(sq_sum_ready, 1)

            def rstd1_of(g):
                need(pool, var1_ready, g + 1)
                need(pool, h1_ready, g)
                nc.gpsimd.tensor_tensor(rstd1[:], var1[:], minus_half[:], ALU.pow).then_inc(rstd1_ready, 1)

            def adjacency_eps(g, parity):
                need_load(pool, adj_loaded, g, parity)
                need(pool, agg_done, g)
                nc.gpsimd.tensor_tensor(adj_eps[:], adj_in[:, parity], eps_eye[:], ALU.add).then_inc(adj_eps_ready, 1)

            def rms_of(g):
                need(pool, ms_eps_ready, g + 1)
                need(pool, diag_ready, g)
                nc.gpsimd.tensor_tensor(rms[:], ms_eps[:], minus_half[:], ALU.pow).then_inc(rms_ready, 1)

            def rstd2_of(g):
                need(pool, var2_ready, g + 1)
                need(pool, h2_nodes_ready, g)
                nc.gpsimd.tensor_tensor(rstd2[:], var2[:], minus_half[:], ALU.pow).then_inc(rstd2_ready, 1)

            def step(t, parity):
                if has(t, -1):
                    blend_inputs(t - 1, 1 - parity)
                if has(t, 1):
                    silu_low(t + 1)
                if has(t, 0):
                    conv2_mix(t, parity)
                if has(t, 3):
                    rstd1_of(t + 3)
                if has(t, 2):
                    square_sum(t + 2)
                if has(t, 1):
                    rstd2_of(t + 1)
                if has(t, 2):
                    rms_of(t + 2)
                if has(t, 3):
                    adjacency_eps(t + 3, 1 - parity)
                if type(t) is int and t == -3:
                    pair_weights()
                    split_low(1)
                if type(t) is int and t == -2:
                    split_low(2)

            steps(pool, step)


def kernel(x, adj, **p):
    import concourse.bacc as bacc
    from concourse.bass_utils import run_bass_kernel_spmd

    def grouped(a, order):
        a = np.asarray(a).reshape(NG, PER, P, P).transpose(0, *(1 + k for k in order))
        return np.ascontiguousarray(a.reshape(NG, P, T))

    arr = {k: np.asarray(a) for k, a in p.items()}
    g1 = lambda name: arr["L1_gnn_" + name]
    w_se = np.zeros((P, P), np.float32)
    bse = np.zeros(P, np.float32)
    for q in range(3):
        w_se[:, 32 * q:32 * q + SEEDS] = g1("w_se").T
        bse[32 * q:32 * q + SEEDS] = g1("b_se")
    parts = {
        "w1": arr["L0_gnn_W1"],
        "conv1": g1("conv1_w")[:, :, 0].T,
        "msg": g1("w_msg").T,
        "se": w_se,
        "hh": g1("w_hh").T,
        "w2": arr["L0_gnn_W2"].reshape(HC, P, P).transpose(1, 0, 2).reshape(P, HC * P),
        "ih": g1("w_ih").reshape(3 * P, 2, P).transpose(2, 1, 0).reshape(P, 6 * P),
        "conv2": g1("conv2_w").transpose(1, 2, 0).reshape(P, TAPS * P),
    }
    weights = np.concatenate([parts[n] for n in W_COLS if n in parts], axis=1)
    vectors = {"bse": bse, "b2": arr["L0_gnn_b2"]}
    for c in range(HC):
        vectors[f"b1_{c}"] = arr["L0_gnn_b1"][c * P:(c + 1) * P]
        vectors[f"rms_{c}"] = arr["L0_gnn_rms_weight"][c * P:(c + 1) * P]
    for n in ("bn1", "bn2"):
        for k in "gbmv":
            vectors[f"{n}_{k}"] = g1(f"{n}_{k}")
    for i, gate in enumerate("rzn"):
        vectors[f"bih_{gate}"] = g1("b_ih")[i * P:(i + 1) * P]
        vectors[f"bhh_{gate}"] = g1("b_hh")[i * P:(i + 1) * P]
    inputs = {
        "x_nodes": grouped(x, (1, 0, 2)),
        "x_feats": grouped(x, (2, 0, 1)),
        "adj_t": grouped(adj, (2, 0, 1)),
        "weights": np.ascontiguousarray(weights),
        "vectors": np.ascontiguousarray(np.stack([vectors[n] for n in V_NAMES], axis=1)),
        "b_msg": np.ascontiguousarray(np.tile(g1("b_msg"), PER)),
        "epsilon": arr["L0_gnn_epsilon"].reshape(1),
    }
    nc = bacc.Bacc("TRN2", target_bir_lowering=False, num_devices=1)
    args = [nc.dram_tensor(n, a.shape, mybir.dt.from_np(a.dtype), kind="ExternalInput").ap() for n, a in inputs.items()]
    out = nc.dram_tensor("out", (NG, P, T), F32, kind="ExternalOutput").ap()
    build(nc, *args, out)
    r = run_bass_kernel_spmd(nc, [inputs], core_ids=[0])
    got = r.results[0]["out"]
    return got.reshape(NG, P, PER, P).transpose(0, 2, 3, 1).reshape(GRAPHS, P, P)
```

```python
from contextlib import ExitStack

import numpy as np

import concourse.bass as bass
from concourse import mybir
from concourse.alu_op_type import AluOpType as ALU

F32 = mybir.dt.float32
F32R = mybir.dt.float32r
ACT = mybir.ActivationFunctionType

P = 128
GRAPHS = 64
PER = 4
T = PER * P
NG = GRAPHS // PER
HC = 4
TAPS = 17
HALF = TAPS // 2
PH = P // 2
PADDED = PH + 4
P1_COLS = PH + 2
LN_EPS, RMS_EPS, BN_EPS = 1e-5, 1e-6, 1e-5
SEEDS = 3
LOOP_FIRST, LOOP_END = 2, 12

W_COLS = {"w1": HC * P, "conv1": P, "se": P, "hh": 3 * P, "w2": HC * P, "ih": 6 * P, "conv2": TAPS * P,
          "conv2_pairs": (TAPS - 1) * P // 2}
W_AT = {}
for _name in W_COLS:
    W_AT[_name] = sum(W_COLS[n] for n in W_AT)
W_TOTAL = sum(W_COLS.values())

V_NAMES = (["b1_0", "b1_1", "b1_2", "b1_3", "rms_0", "rms_1", "rms_2", "rms_3", "b2",
            "dist_l_scale", "dist_l_bias", "dist_r_scale", "dist_r_bias",
            "bn1_g", "bn2_g", "bn1_b", "bn2_b", "bn1_m", "bn2_m", "bn1_v", "bn2_v",
            "bih_r", "bih_z", "bih_n", "bhh_r", "bhh_z", "bhh_n"])
V_AT = {n: i for i, n in enumerate(V_NAMES)}


def build(nc, x_nodes, x_feats, adj_t, weights, w_msg, vectors, b_msg, epsilon, out):
    with ExitStack() as ctx:
        def sb(name, shape, dt=F32):
            return ctx.enter_context(nc.sbuf_tensor(name, shape, dt))

        def sem(name):
            return ctx.enter_context(nc.semaphore(name))

        w_hi = sb("w_hi", [P, W_TOTAL], F32R)
        w_lo = sb("w_lo", [P, W_TOTAL], F32R)
        late_tiles = sb("late_tiles", [P, 15, T])
        assert W_TOTAL <= 15 * T
        w_raw = late_tiles[:].rearrange("p i t -> p (i t)")[:, 0:W_TOTAL]
        (tanh_r, tanh_z, gh_n, r_gh, n_in, n_gate, h_minus_n, x1_plus_n, z_part, conv_sum,
         xc, out_sb) = (late_tiles[:, i] for i in range(12))
        exp_dist, kernel_a, msg = (late_tiles[:, i].rearrange("p (g n) -> p g n", g=PER) for i in range(12, 15))
        vec = sb("vec", [P, len(V_NAMES)])
        w_msg_sb = sb("w_msg_sb", [P, P])
        b_msg_sb = sb("b_msg_sb", [P, PER, P])
        eps_col = sb("eps_col", [P, 1])
        eye = sb("eye", [P, P])
        eps_eye = sb("eps_eye", [P, PER, P])
        ones = sb("ones", [P, P], F32R)
        zeros = sb("zeros", [P, T], F32R)
        minus_half = sb("minus_half", [P, PER])
        hb_bias = sb("hb_bias", [P, HC])
        bn_scale = sb("bn_scale", [P, 2])
        bn2_minus = sb("bn2_minus", [P, 1])
        bn_root = sb("bn_root", [P, 2])
        table_use = sb("table_use", [P, 2])
        bn_inv = sb("bn_inv", [P, 2])
        bn_ms = sb("bn_ms", [P, 2])
        bn_bias = sb("bn_bias", [P, 2])
        gate_sum = sb("gate_sum", [P, 2])
        gate_bias = sb("gate_bias", [P, 2])

        x_in = sb("x_in", [P, 2, PER, P])
        adj_in = sb("adj_in", [P, 2, PER, P])
        xT_in = sb("xT_in", [P, 2, T])
        mask_in = sb("mask_in", [P, 2, PER, P])
        stats1 = sb("stats1", [P, PER, 6])
        moments1 = sb("moments1", [P, PER, 2])
        var1 = sb("var1", [P, PER])
        rstd1 = sb("rstd1", [P, PER])
        shift1 = sb("shift1", [P, PER])
        h1 = sb("h1", [P, PER, P])
        adj_eps = sb("adj_eps", [P, PER, P])
        agg_hi = sb("agg_hi", [P, T], F32R)
        agg_lo = sb("agg_lo", [P, T], F32R)
        sq = sb("sq", [P, HC, T])
        hb = sb("hb", [P, 2, HC, T])
        sq_total = sb("sq_total", [P, PER])
        ms_eps = sb("ms_eps", [P, PER])
        rms = sb("rms", [P, PER])
        v = sb("v", [P, 2, T])
        tanh_v = sb("tanh_v", [P, 2, T])
        silu = sb("silu", [P, 2, T])
        silu_hi = sb("silu_hi", [P, HC, T], F32R)
        silu_lo = sb("silu_lo", [P, HC, T], F32R)
        x1 = sb("x1", [P, 2, T])
        stats2 = sb("stats2", [P, PER, 6])
        moments2 = sb("moments2", [P, PER, 2])
        var2 = sb("var2", [P, PER])
        rstd2 = sb("rstd2", [P, PER])
        shift2 = sb("shift2", [P, PER])
        h2_nodes = sb("h2_nodes", [P, PER, P])
        h2 = sb("h2", [P, 2, T])
        h2_hi = sb("h2_hi", [P, T], F32R)
        h2_lo = sb("h2_lo", [P, T], F32R)
        c1 = sb("c1", [P, 3, PER, PH])
        c1_hi = sb("c1_hi", [P, 3, PER, PADDED], F32R)
        c1_lo = sb("c1_lo", [P, 3, PER, PADDED], F32R)
        p1 = sb("p1", [P, PER, P1_COLS])
        mix_even = sb("mix_even", [P, PER, PH])
        mix_odd = sb("mix_odd", [P, PER, PH])
        even_part = sb("even_part", [P, PER * PH])
        dist_l = sb("dist_l", [96, T])
        dist_r = sb("dist_r", [96, T])
        nmp_hi = sb("nmp_hi", [P, T], F32R)
        nmp_lo = sb("nmp_lo", [P, T], F32R)
        xc_hi = sb("xc_hi", [P, T], F32R)
        xc_lo = sb("xc_lo", [P, T], F32R)

        bank = [ctx.enter_context(nc.psum_tensor(f"bank{i}", [P, T], F32)) for i in range(8)]
        conv2_p0, conv2_p2 = bank[0][:, 0:PER * PH], bank[0][:, PER * PH:T]
        conv2_p1 = bank[2][:, 0:PER * P1_COLS]
        conv1_ps = agg_ps = dist_ps = x1_nodes_ps = bank[1]
        seed_ps = w2_ps = sq_nodes_ps = bank[2]
        msg_ps = nmp_ps = h2_ps = bank[3]
        rms_ps = r_ps = bank[4]
        z_ps, hn_ps, in_ps = bank[5], bank[6], bank[7]
        w1_ps = [bank[3], bank[5], bank[6], bank[7]]

        LOTS = ("w1", "layer1", "ih", "conv2", "pairs")
        raw_ready = {lot: sem(f"raw_{lot}_ready") for lot in LOTS}
        hi_ready = {lot: sem(f"hi_{lot}_ready") for lot in LOTS}
        lo_ready = {lot: sem(f"lo_{lot}_ready") for lot in LOTS}
        small_loaded, b_msg_loaded, w_msg_loaded = sem("small_loaded"), sem("b_msg_loaded"), sem("w_msg_loaded")
        const_ready, eye_zeroed, eye_ready = sem("const_ready"), sem("eye_zeroed"), sem("eye_ready")
        eps_eye_ready = sem("eps_eye_ready")
        prep, root_ready = sem("prep"), sem("root_ready")
        x_loaded = [sem(f"x_loaded{i}") for i in range(2)]
        adj_loaded = [sem(f"adj_loaded{i}") for i in range(2)]
        xT_loaded = [sem(f"xT_loaded{i}") for i in range(2)]
        mask_loaded = [sem(f"mask_loaded{i}") for i in range(2)]
        stats1_ready, moments1_ready, var1_ready = sem("stats1_ready"), sem("moments1_ready"), sem("var1_ready")
        rstd1_ready, shift1_ready = sem("rstd1_ready"), sem("shift1_ready")
        h1_ready, adj_eps_ready = sem("h1_ready"), sem("adj_eps_ready")
        agg_done, agg_hi_ready, agg_lo_ready = sem("agg_done"), sem("agg_hi_ready"), sem("agg_lo_ready")
        w1_done = [sem(f"w1_done{c}") for c in range(HC)]
        sq_ready = [sem(f"sq_ready{c}") for c in range(HC)]
        hb_ready = [sem(f"hb_ready{c}") for c in range(HC)]
        sq_pairs, sq_sum_ready = sem("sq_pairs"), sem("sq_sum_ready")
        sq_nodes_done, sq_total_ready = sem("sq_nodes_done"), sem("sq_total_ready")
        ms_eps_ready, rms_ready = sem("ms_eps_ready"), sem("rms_ready")
        rms_done = sem("rms_done")
        v_ready = [sem(f"v_ready{c}") for c in range(HC)]
        tanh_ready = [sem(f"tanh_ready{c}") for c in range(HC)]
        silu_ready = [sem(f"silu_ready{c}") for c in range(HC)]
        silu_hi_ready = [sem(f"silu_hi_ready{c}") for c in range(HC)]
        silu_lo_ready = [sem(f"silu_lo_ready{c}") for c in range(HC)]
        w2_done, x1_ready, x1_nodes_done = sem("w2_done"), sem("x1_ready"), sem("x1_nodes_done")
        stats2_ready, moments2_ready, var2_ready = sem("stats2_ready"), sem("moments2_ready"), sem("var2_ready")
        rstd2_ready, shift2_ready, h2_nodes_ready = sem("rstd2_ready"), sem("shift2_ready"), sem("h2_nodes_ready")
        h2_done, h2_ready = sem("h2_done"), sem("h2_ready")
        h2_hi_ready, h2_lo_ready = sem("h2_hi_ready"), sem("h2_lo_ready")
        conv1_done, c1_ready = sem("conv1_done"), sem("c1_ready")
        c1_hi_ready, c1_lo_ready = sem("c1_hi_ready"), sem("c1_lo_ready")
        seed_done, dist_ops_ready, dist_done, a_ready = sem("seed_done"), sem("dist_ops_ready"), sem("dist_done"), sem("a_ready")
        exp_ready, dist_squares_ready = sem("exp_ready"), sem("dist_squares_ready")
        msg_done, msg_sum_ready, msg_ready = sem("msg_done"), sem("msg_sum_ready"), sem("msg_ready")
        nmp_done, nmp_hi_ready, nmp_lo_ready = sem("nmp_done"), sem("nmp_hi_ready"), sem("nmp_lo_ready")
        c1_sum_ready = sem("c1_sum_ready")
        c1_sum_hi_ready, c1_sum_lo_ready = sem("c1_sum_hi_ready"), sem("c1_sum_lo_ready")
        p1_done, p1_ready, mix_ready, even_part_ready = sem("p1_done"), sem("p1_ready"), sem("mix_ready"), sem("even_part_ready")
        conv2_done, conv_sum_ready, xc_ready = sem("conv2_done"), sem("conv_sum_ready"), sem("xc_ready")
        xc_hi_ready, xc_lo_ready = sem("xc_hi_ready"), sem("xc_lo_ready")
        r_done, z_done, hn_done, in_done = sem("r_done"), sem("z_done"), sem("hn_done"), sem("in_done")
        tanh_r_ready, tanh_z_ready, gh_n_ready = sem("tanh_r_ready"), sem("tanh_z_ready"), sem("gh_n_ready")
        r_gh_ready, n_in_ready, n_ready = sem("r_gh_ready"), sem("n_in_ready"), sem("n_ready")
        h_minus_n_ready, x1_plus_n_ready = sem("h_minus_n_ready"), sem("x1_plus_n_ready")
        z_part_ready, out_ready, stored = sem("z_part_ready"), sem("out_ready"), sem("stored")

        def need(eng, semaphore, groups):
            if type(groups) is int:
                if groups <= 0:
                    return
                groups = min(groups, NG)
            eng.wait_ge(semaphore, groups)

        def need_load(eng, semaphores, g, parity):
            eng.wait_ge(semaphores[parity], g * 8 + (16 - 8 * parity))

        def steps(eng, step, first=-3, last=NG):
            for t in range(first, LOOP_FIRST):
                step(t, t % 2)
            with eng.Fori(LOOP_FIRST, LOOP_END, 2) as t:
                for k in range(2):
                    step(t + k if k else t, (LOOP_FIRST + k) % 2)
            for t in range(LOOP_END, last + 1):
                step(t, t % 2)

        def has(t, lag):
            return type(t) is not int or 0 <= t + lag < NG

        def peeled(t, step):
            return type(t) is int and t == step

        def w(part, name, block):
            at = W_AT[name] + block * P
            return part[:, at:at + P]

        def bias(name):
            return vec[:, V_AT[name]:V_AT[name] + 1]

        def cols(name, n):
            return vec[:, V_AT[name]:V_AT[name] + n]

        def graph(j):
            return slice(j * P, (j + 1) * P)

        lot_ends = [W_AT["conv1"], W_AT["ih"], W_AT["conv2"], W_AT["conv2_pairs"], W_TOTAL]
        lot_cols = {lot: slice(a, b) for lot, a, b in zip(LOTS, [0] + lot_ends, lot_ends)}

        block = ctx.enter_context(nc.Block())

        @block.sync
        def _(sp):
            def load_x(g, parity):
                need(sp, h1_ready, g - 1)
                sp.dma_start(x_in[:, parity], x_nodes[g]).then_inc(x_loaded[parity], 16)
                need(sp, adj_eps_ready, g - 1)
                sp.dma_start(adj_in[:, parity], adj_t[g]).then_inc(adj_loaded[parity], 16)

            def load_xT(g, parity):
                need(sp, x1_ready, g - 1)
                sp.dma_start(xT_in[:, parity], x_feats[g]).then_inc(xT_loaded[parity], 16)

            def load_mask(g, parity):
                need(sp, a_ready, g - 1)
                sp.dma_start(mask_in[:, parity], adj_t[g]).then_inc(mask_loaded[parity], 16)

            def store(g):
                sp.wait_ge(out_ready, g + 1)
                sp.dma_start(out[g], out_sb).then_inc(stored, 16)

            def load_weights(lot):
                at = lot_cols[lot]
                sp.dma_start(w_raw[:, at], weights[:, at]).then_inc(raw_ready[lot], 16)

            sp.dma_start(x_in[:, 0], x_nodes[0]).then_inc(x_loaded[0], 16)
            sp.dma_start(vec[:], vectors).then_inc(small_loaded, 16)
            sp.dma_start(eps_col[:], epsilon.partition_broadcast(P)).then_inc(small_loaded, 16)
            load_weights("w1")
            sp.dma_start(adj_in[:, 0], adj_t[0]).then_inc(adj_loaded[0], 16)
            load_x(1, 1)
            load_weights("layer1")
            load_weights("conv2")
            sp.dma_start(w_msg_sb[:], w_msg).then_inc(w_msg_loaded, 16)
            sp.dma_start(b_msg_sb[:], b_msg.partition_broadcast(P)).then_inc(b_msg_loaded, 16)
            load_weights("ih")
            load_xT(0, 0)
            load_xT(1, 1)

            def step(t, parity):
                if has(t, 4) and not (type(t) is int and t < -2):
                    load_x(t + 4, parity)
                if has(t, 2) and not (type(t) is int and t < 0):
                    load_xT(t + 2, parity)
                if has(t, 1):
                    load_mask(t + 1, 1 - parity)
                if has(t, -1):
                    store(t - 1)

            for t in range(-2, 1):
                step(t, t % 2)
            with sp.Fori(1, 11, 2) as t:
                for k in range(2):
                    step(t + k if k else t, (1 + k) % 2)
            for t in range(11, NG + 1):
                step(t, t % 2)
            sp.wait_ge(stored, 16 * NG)

        @block.tensor
        def _(pe):
            def exact(out_ps, name, block_, hi, lo, first, last):
                with_high(out_ps, name, block_, hi, first)
                return with_low(out_ps, name, block_, lo, last)

            def with_high(out_ps, name, block_, hi, first):
                nc.tensor.matmul(out_ps, w(w_hi, name, block_), hi, start=first, stop=False)
                nc.tensor.matmul(out_ps, w(w_lo, name, block_), hi, start=False, stop=False)

            def with_low(out_ps, name, block_, lo, last):
                return nc.tensor.matmul(out_ps, w(w_hi, name, block_), lo, start=False, stop=last)

            def keep_warm(products):
                for _ in range(products):
                    nc.tensor.matmul(bank[0][:], ones[:], zeros[:], start=True, stop=True)

            def weights_split(lot):
                pe.wait_ge(hi_ready[lot], 1)
                pe.wait_ge(lo_ready[lot], 1)

            def conv1(g):
                pe.wait_ge(h2_hi_ready, g + 1)
                with_high(conv1_ps[:], "conv1", 0, h2_hi[:], True)
                pe.wait_ge(h2_lo_ready, g + 1)
                with_low(conv1_ps[:], "conv1", 0, h2_lo[:], True).then_inc(conv1_done, 1)

            def seeds(g):
                need(pe, sq_total_ready, g + 2)
                exact(seed_ps[:], "se", 0, h2_hi[:], h2_lo[:], True, True).then_inc(seed_done, 1)

            def messages(g, parity):
                pe.wait_ge(h2_ready, g + 1)
                for j in range(PER):
                    last = nc.tensor.matmul(msg_ps[:, graph(j)], h2[:, parity, graph(j)], w_msg_sb[:], start=True, stop=True)
                last.then_inc(msg_done, 1)

            def aggregate(g):
                pe.wait_ge(h1_ready, g + 1)
                pe.wait_ge(adj_eps_ready, g + 1)
                need(pe, c1_ready, g - 1)
                for j in range(PER):
                    last = nc.tensor.matmul(agg_ps[:, graph(j)], h1[:, j], adj_eps[:, j], start=True, stop=True)
                last.then_inc(agg_done, 1)

            def rms_rows(g):
                pe.wait_ge(rms_ready, g + 1)
                need(pe, tanh_r_ready, g - 1)
                for j in range(PER):
                    last = nc.tensor.transpose(rms_ps[:, graph(j)], rms[:, j:j + 1].to_broadcast([P, P]), eye[:])
                last.then_inc(rms_done, 1)

            def w1(g):
                pe.wait_ge(agg_hi_ready, g + 1)
                pe.wait_ge(agg_lo_ready, g + 1)
                for c, (semaphore, groups) in enumerate(((msg_sum_ready, g - 1), (tanh_z_ready, g - 2),
                                                         (gh_n_ready, g - 2), (n_in_ready, g - 2))):
                    need(pe, semaphore, groups)
                    exact(w1_ps[c][:], "w1", c, agg_hi[:], agg_lo[:], True, True).then_inc(w1_done[c], 1)

            def distances(g):
                pe.wait_ge(dist_squares_ready, g + 1)
                need(pe, agg_hi_ready, g + 3)
                need(pe, agg_lo_ready, g + 3)
                for j in range(PER):
                    last = nc.tensor.matmul(dist_ps[:, graph(j)], dist_l[:, graph(j)], dist_r[:, graph(j)],
                                            start=True, stop=True)
                last.then_inc(dist_done, 1)

            def half_conv(out_ps, width, phase, tap_blocks, parts):
                n_taps = len(tap_blocks)
                order = sorted(range(n_taps), key=lambda k: abs(k - HALF // 2))
                for k in order[parts]:
                    s = k - HALF // 2
                    a = max(0, -s) & ~1
                    b = width if k == order[0] else min(width, (PH - s + 1) & ~1)
                    hi, lo = (c[:, phase, :, a + s + 1:b + s + 1] for c in (c1_hi, c1_lo))
                    last = exact(out_ps[:, :, a:b], *tap_blocks[k], hi, lo, k == order[0], k == order[-1])
                return last

            even_taps = [("conv2", 2 * a) for a in range(HALF + 1)]
            odd_taps = [("conv2", 2 * a + 1) for a in range(HALF)]
            pair_taps = [("conv2_pairs", a) for a in range(HALF)] + [("conv2", TAPS - 1)]

            def conv2_p1_product(g, parts):
                pe.wait_ge(c1_hi_ready, g + 1)
                pe.wait_ge(c1_lo_ready, g + 1)
                pe.wait_ge(dist_ops_ready, g + 1)
                return half_conv(conv2_p1.rearrange("p (g n) -> p g n", g=PER), P1_COLS, 0, odd_taps,
                                 parts)

            def conv2_p0_product(g):
                need(pe, conv_sum_ready, g)
                half_conv(conv2_p0.rearrange("p (g n) -> p g n", g=PER), PH, 1, even_taps, slice(None))

            def conv2_p2_product(g, parts):
                pe.wait_ge(c1_sum_hi_ready, g + 1)
                pe.wait_ge(c1_sum_lo_ready, g + 1)
                return half_conv(conv2_p2.rearrange("p (g n) -> p g n", g=PER), PH, 2, pair_taps, parts)

            def w2(g, c):
                if c == 0:
                    need(pe, p1_ready, g)
                pe.wait_ge(silu_hi_ready[c], g + 1)
                pe.wait_ge(silu_lo_ready[c], g + 1)
                last = exact(w2_ps[:], "w2", c, silu_hi[:, c], silu_lo[:, c], c == 0, c == HC - 1)
                if c == HC - 1:
                    last.then_inc(w2_done, 1)

            def gather(g):
                pe.wait_ge(a_ready, g + 1)
                pe.wait_ge(msg_ready, g + 1)
                need(pe, sq_ready[0], g + 3)
                need(pe, hb_ready[0], g + 3)
                for j in range(PER):
                    last = nc.tensor.matmul(nmp_ps[:, graph(j)], msg[:, j], kernel_a[:, j], start=True, stop=True)
                last.then_inc(nmp_done, 1)

            def x1_by_nodes(g, parity):
                pe.wait_ge(x1_ready, g + 1)
                need(pe, exp_ready, g)
                for j in range(PER):
                    last = nc.tensor.transpose(x1_nodes_ps[:, graph(j)], x1[:, parity, graph(j)], eye[:])
                last.then_inc(x1_nodes_done, 1)

            def squares_by_nodes(g):
                pe.wait_ge(sq_sum_ready, g + 1)
                need(pe, x1_ready, g)
                for j in range(PER):
                    last = nc.tensor.transpose(sq_nodes_ps[:, graph(j)], sq[:, 0, graph(j)], eye[:])
                last.then_inc(sq_nodes_done, 1)

            def h2_by_features(g):
                pe.wait_ge(h2_nodes_ready, g + 1)
                need(pe, nmp_hi_ready, g)
                need(pe, nmp_lo_ready, g)
                for j in range(PER):
                    last = nc.tensor.transpose(h2_ps[:, graph(j)], h2_nodes[:, j], eye[:])
                last.then_inc(h2_done, 1)

            def gates_early(g):
                pe.wait_ge(nmp_hi_ready, g + 1)
                pe.wait_ge(nmp_lo_ready, g + 1)
                need(pe, v_ready[HC - 1], g + 2)
                exact(r_ps[:], "hh", 0, h2_hi[:], h2_lo[:], True, False)
                exact(r_ps[:], "ih", 3, nmp_hi[:], nmp_lo[:], False, False)
                for c in range(1, HC):
                    need(pe, sq_ready[c], g + 3)
                    need(pe, hb_ready[c], g + 3)
                exact(z_ps[:], "hh", 1, h2_hi[:], h2_lo[:], True, False)
                exact(z_ps[:], "ih", 4, nmp_hi[:], nmp_lo[:], False, False)
                exact(hn_ps[:], "hh", 2, h2_hi[:], h2_lo[:], True, True).then_inc(hn_done, 1)
                exact(in_ps[:], "ih", 5, nmp_hi[:], nmp_lo[:], True, False)

            def gates_late(g):
                pe.wait_ge(xc_hi_ready, g + 1)
                with_high(r_ps[:], "ih", 0, xc_hi[:], False)
                pe.wait_ge(xc_lo_ready, g + 1)
                with_low(r_ps[:], "ih", 0, xc_lo[:], True).then_inc(r_done, 1)
                exact(in_ps[:], "ih", 2, xc_hi[:], xc_lo[:], False, True).then_inc(in_done, 1)
                exact(z_ps[:], "ih", 1, xc_hi[:], xc_lo[:], False, True).then_inc(z_done, 1)

            def step(t, parity):
                if has(t, 0):
                    if peeled(t, 0):
                        weights_split("conv2")
                    conv1(t)
                    seeds(t)
                    if peeled(t, 0):
                        pe.wait_ge(w_msg_loaded, 16)
                    messages(t, parity)
                if has(t, 2):
                    if peeled(t, -2):
                        pe.wait_ge(eye_ready, 1)
                        pe.wait_ge(const_ready, 1)
                    aggregate(t + 2)
                    if peeled(t, -2):
                        weights_split("w1")
                    if peeled(t, -1):
                        keep_warm(4)
                if has(t, 0):
                    conv2_p1_product(t, slice(0, 3))
                if has(t, 1):
                    rms_rows(t + 1)
                if has(t, 0):
                    conv2_p1_product(t, slice(3, None)).then_inc(p1_done, 1)
                    distances(t)
                if has(t, 2):
                    w1(t + 2)
                if peeled(t, -2):
                    keep_warm(16)
                if has(t, 0):
                    conv2_p0_product(t)
                if has(t, 1):
                    if peeled(t, -1):
                        weights_split("layer1")
                    w2(t + 1, 0)
                    w2(t + 1, 1)
                if has(t, 0):
                    gather(t)
                if has(t, 1):
                    w2(t + 1, 2)
                    w2(t + 1, 3)
                if has(t, 0):
                    if peeled(t, 0):
                        weights_split("pairs")
                        weights_split("ih")
                    conv2_p2_product(t, slice(0, 6))
                if has(t, 1):
                    x1_by_nodes(t + 1, 1 - parity)
                if has(t, 0):
                    conv2_p2_product(t, slice(6, None)).then_inc(conv2_done, 1)
                    gates_early(t)
                if has(t, 2) and not peeled(t, -1):
                    squares_by_nodes(t + 2)
                if has(t, 1):
                    if peeled(t, -1):
                        keep_warm(18)
                    h2_by_features(t + 1)
                if peeled(t, -1):
                    squares_by_nodes(t + 2)
                if has(t, 0):
                    gates_late(t)

            pe.wait_ge(const_ready, 1)
            keep_warm(16)
            steps(pe, step)

        @block.scalar
        def _(act):
            act.wait_ge(prep, 1)
            nc.scalar.activation(bn_root[:], bn_root[:], ACT.Sqrt).then_inc(root_ready, 1)

            nc.scalar.activation(table_use[:], vec[:, 0:2], ACT.Tanh)

            def split_high(lot):
                act.wait_ge(raw_ready[lot], 16 if lot != "pairs" else 1)
                nc.scalar.copy(w_hi[:, lot_cols[lot]], w_raw[:, lot_cols[lot]]).then_inc(hi_ready[lot], 1)

            split_high("w1")

            def r_and_z(g):
                act.wait_ge(hn_done, g + 1)
                need(act, r_gh_ready, g)
                nc.scalar.activation(gh_n, hn_ps[:], ACT.Identity, bias=bias("bhh_n")).then_inc(gh_n_ready, 1)
                act.wait_ge(r_done, g + 1)
                nc.scalar.activation(tanh_r, r_ps[:], ACT.Tanh, bias=gate_bias[:, 0:1], scale=0.5).then_inc(tanh_r_ready, 1)
                act.wait_ge(z_done, g + 1)
                need(act, z_part_ready, g)
                nc.scalar.activation(tanh_z, z_ps[:], ACT.Tanh, bias=gate_bias[:, 1:2], scale=0.5).then_inc(tanh_z_ready, 1)

            def n_of(g):
                act.wait_ge(n_in_ready, g + 1)
                need(act, h_minus_n_ready, g)
                need(act, x1_plus_n_ready, g)
                nc.scalar.activation(n_gate, n_in, ACT.Tanh, bias=bias("bih_n")).then_inc(n_ready, 1)

            def conv1_relu(g):
                act.wait_ge(conv1_done, g + 1)
                need(act, c1_lo_ready, g)
                need(act, c1_sum_ready, g)
                nc.scalar.activation(c1[:, 0:2].rearrange("p ph g i -> p g i ph"),
                                     conv1_ps[:].rearrange("p (g i ph) -> p g i ph", g=PER, ph=2), ACT.Relu,
                                     bias=bn_bias[:, 0:1], scale=bn_scale[:, 0:1]).then_inc(c1_ready, 1)

            def distance_operands(g):
                act.wait_ge(seed_done, g + 1)
                need(act, dist_done, g)
                nc.scalar.activation(dist_l[:], seed_ps[0:96], ACT.Identity, bias=bias("dist_l_bias")[0:96],
                                     scale=bias("dist_l_scale")[0:96])
                nc.scalar.activation(dist_r[:], seed_ps[0:96], ACT.Identity, bias=bias("dist_r_bias")[0:96],
                                     scale=bias("dist_r_scale")[0:96]).then_inc(dist_ops_ready, 1)
                act.wait_ge(dist_ops_ready, g + 1)
                nc.scalar.activation(dist_l[32:64], dist_l[32:64], ACT.Square)
                nc.scalar.activation(dist_r[64:96], dist_r[64:96], ACT.Square).then_inc(dist_squares_ready, 1)

            def aggregate_high(g):
                act.wait_ge(agg_done, g + 1)
                need(act, w1_done[HC - 1], g)
                nc.scalar.copy(agg_hi[:], agg_ps[:]).then_inc(agg_hi_ready, 1)

            def p1_scaled(g):
                act.wait_ge(p1_done, g + 1)
                need(act, mix_ready, g)
                nc.scalar.activation(p1[:].rearrange("p g n -> p (g n)"), conv2_p1, ACT.Identity,
                                     scale=bn_scale[:, 1:2]).then_inc(p1_ready, 1)

            def silu_tanh(g, chunks):
                for c in chunks:
                    act.wait_ge(v_ready[c], g + 1)
                    need(act, silu_ready[(c + 2) % HC], g + (1 if c >= 2 else 0))
                    nc.scalar.activation(tanh_v[:, c % 2], v[:, c % 2], ACT.Tanh).then_inc(tanh_ready[c], 1)

            def scaled(parity, c):
                nc.scalar.activation(hb[:, parity, c], w1_ps[c][:], ACT.Identity, bias=hb_bias[:, c:c + 1],
                                     scale=bias(f"rms_{c}")).then_inc(hb_ready[c], 1)

            def hidden(g, parity, squares_first):
                for c in range(HC):
                    act.wait_ge(w1_done[c], g + 1)
                    if c == 0:
                        need(act, sq_nodes_done, g)
                        need(act, v_ready[HC - 1], g - 1)
                    nc.scalar.activation(sq[:, c], w1_ps[c][:], ACT.Square, bias=bias(f"b1_{c}")).then_inc(sq_ready[c], 1)
                    if not squares_first:
                        scaled(parity, c)
                for c in range(HC if squares_first else 0):
                    scaled(parity, c)

            def exponential(g):
                act.wait_ge(dist_done, g + 1)
                need(act, a_ready, g)
                nc.scalar.activation(exp_dist.rearrange("p g n -> p (g n)"), dist_ps[:], ACT.Exp, scale=2.0).then_inc(
                    exp_ready, 1)

            def layernorm1_relu(g, parity):
                act.wait_ge(shift1_ready, g + 1)
                need(act, agg_done, g)
                for j in range(PER):
                    last = nc.scalar.activation(h1[:, j], x_in[:, parity, j], ACT.Relu, bias=shift1[:, j:j + 1],
                                                scale=rstd1[:, j:j + 1])
                last.then_inc(h1_ready, 1)

            def gathered_high(g):
                act.wait_ge(nmp_done, g + 1)
                need(act, in_done, g)
                nc.scalar.copy(nmp_hi[:], nmp_ps[:]).then_inc(nmp_hi_ready, 1)

            def layernorm2_relu(g):
                act.wait_ge(shift2_ready, g + 1)
                need(act, h2_done, g)
                for j in range(PER):
                    last = nc.scalar.activation(h2_nodes[:, j], x1_nodes_ps[:, graph(j)], ACT.Relu,
                                                bias=shift2[:, j:j + 1], scale=rstd2[:, j:j + 1])
                last.then_inc(h2_nodes_ready, 1)

            def h2_full(g, parity):
                act.wait_ge(h2_done, g + 1)
                need(act, hn_done, g)
                nc.scalar.copy(h2_hi[:], h2_ps[:]).then_inc(h2_hi_ready, 1)
                need(act, h_minus_n_ready, g - 1)
                nc.scalar.copy(h2[:, parity], h2_ps[:]).then_inc(h2_ready, 1)

            def step(t, parity):
                if has(t, -1):
                    r_and_z(t - 1)
                if has(t, 0):
                    conv1_relu(t)
                    distance_operands(t)
                if has(t, 2):
                    aggregate_high(t + 2)
                if has(t, -1):
                    n_of(t - 1)
                if has(t, 1):
                    silu_tanh(t + 1, (0, 1))
                if has(t, 0):
                    p1_scaled(t)
                if has(t, 1):
                    silu_tanh(t + 1, (2,))
                if has(t, 0):
                    exponential(t)
                if has(t, 1):
                    silu_tanh(t + 1, (3,))
                if has(t, 2):
                    if peeled(t, -2):
                        act.wait_ge(prep, 10)
                    hidden(t + 2, parity, peeled(t, -2))
                if has(t, 0):
                    gathered_high(t)
                if has(t, 3):
                    layernorm1_relu(t + 3, 1 - parity)
                if peeled(t, -3):
                    split_high("layer1")
                if peeled(t, -2):
                    split_high("ih")
                if peeled(t, -1):
                    split_high("pairs")
                if has(t, 1):
                    layernorm2_relu(t + 1)
                    h2_full(t + 1, 1 - parity)

            steps(act, step)

        @block.vector
        def _(dve):
            done = [0]

            def chained(ins):
                done[0] += 1
                ins.then_inc(prep, 1)
                dve.wait_ge(prep, done[0])

            for phase in range(3):
                for c in (c1_hi, c1_lo):
                    nc.vector.memset(c[:, phase, :, 0:1].bitcast(F32), 0.0)
                    nc.vector.memset(c[:, phase, :, PH + 1:PADDED].bitcast(F32), 0.0)
            nc.vector.memset(minus_half[:], -0.5)
            nc.vector.memset(zeros[:].bitcast(F32), 0.0)
            nc.vector.memset(ones[:].bitcast(F32), 1.0).then_inc(const_ready, 1)
            dve.wait_ge(small_loaded, 32)
            chained(nc.vector.tensor_scalar(bn_root[:], cols("bn1_v", 2), BN_EPS, None, ALU.add))

            def derived_vectors():
                chained(nc.vector.tensor_scalar(cols("rms_0", HC), cols("rms_0", HC), 0.5, None, ALU.mult))
                chained(nc.vector.tensor_tensor(hb_bias[:], cols("b1_0", HC), cols("rms_0", HC), ALU.mult))
                chained(nc.vector.tensor_tensor(gate_sum[:], cols("bih_r", 2), cols("bhh_r", 2), ALU.add))
                chained(nc.vector.tensor_scalar(gate_bias[:], gate_sum[:], 0.5, None, ALU.mult))
                dve.wait_ge(root_ready, 1)
                chained(nc.vector.reciprocal(bn_inv[:], bn_root[:]))
                chained(nc.vector.tensor_tensor(bn_scale[:], bn_inv[:], cols("bn1_g", 2), ALU.mult))
                chained(nc.vector.tensor_tensor(bn_ms[:], bn_scale[:], cols("bn1_m", 2), ALU.mult))
                chained(nc.vector.tensor_tensor(bn_bias[:], cols("bn1_b", 2), bn_ms[:], ALU.subtract))
                chained(nc.vector.tensor_scalar(bn2_minus[:], bn_scale[:, 1:2], -1.0, None, ALU.mult))

            def epsilon_identity():
                dve.wait_ge(eye_ready, 1)
                for j in range(PER):
                    last = nc.vector.tensor_scalar(eps_eye[:, j], eye[:], eps_col[:, 0:1], None, ALU.mult)
                last.then_inc(eps_eye_ready, 1)

            def split_low(lot):
                dve.wait_ge(hi_ready[lot], 1)
                nc.vector.tensor_tensor(w_lo[:, lot_cols[lot]], w_raw[:, lot_cols[lot]], w_hi[:, lot_cols[lot]].bitcast(F32),
                                        ALU.subtract).then_inc(lo_ready[lot], 1)

            def split_high(lot):
                dve.wait_ge(raw_ready[lot], 16)
                nc.vector.tensor_copy(w_hi[:, lot_cols[lot]], w_raw[:, lot_cols[lot]]).then_inc(hi_ready[lot], 1)

            def reset_and_input(g):
                dve.wait_ge(tanh_r_ready, g + 1)
                dve.wait_ge(gh_n_ready, g + 1)
                need(dve, n_in_ready, g)
                nc.vector.scalar_tensor_tensor(r_gh, tanh_r, 1.0, gh_n, ALU.add, ALU.mult).then_inc(r_gh_ready, 1)
                dve.wait_ge(r_gh_ready, g + 1)
                dve.wait_ge(in_done, g + 1)
                need(dve, n_ready, g)
                nc.vector.scalar_tensor_tensor(n_in, r_gh, 0.5, in_ps[:], ALU.mult, ALU.add).then_inc(n_in_ready, 1)

            def interior(padded, a, b):
                return padded[:, a:b].rearrange("p ph g i -> p (ph g) i")[:, :, 1:PH + 1]

            def by_graph(phases, a, b):
                return phases[:, a:b].rearrange("p ph g i -> p (ph g) i")

            def conv1_split(g):
                dve.wait_ge(c1_ready, g + 1)
                need(dve, conv2_done, g)
                nc.vector.tensor_copy(interior(c1_hi, 0, 2), by_graph(c1, 0, 2)).then_inc(c1_hi_ready, 1)
                dve.wait_ge(c1_hi_ready, g + 1)
                nc.vector.tensor_tensor(interior(c1_lo, 0, 2), by_graph(c1, 0, 2), interior(c1_hi, 0, 2).bitcast(F32),
                                        ALU.subtract).then_inc(c1_lo_ready, 1)

            def conv1_sum_split(g):
                need(dve, c1_sum_lo_ready, g)
                nc.vector.tensor_tensor(c1[:, 2], c1[:, 0], c1[:, 1], ALU.add).then_inc(c1_sum_ready, 1)
                dve.wait_ge(c1_sum_ready, g + 1)
                nc.vector.tensor_copy(interior(c1_hi, 2, 3), by_graph(c1, 2, 3)).then_inc(c1_sum_hi_ready, 1)
                dve.wait_ge(c1_sum_hi_ready, g + 1)
                nc.vector.tensor_tensor(interior(c1_lo, 2, 3), by_graph(c1, 2, 3), interior(c1_hi, 2, 3).bitcast(F32),
                                        ALU.subtract).then_inc(c1_sum_lo_ready, 1)

            def message_bias(g):
                dve.wait_ge(msg_done, g + 1)
                need(dve, nmp_done, g)
                nc.vector.tensor_tensor(msg, msg_ps[:].rearrange("p (g n) -> p g n", n=P), b_msg_sb[:],
                                        ALU.add).then_inc(msg_sum_ready, 1)

            def message_relu(g):
                dve.wait_ge(msg_sum_ready, g + 1)
                nc.vector.tensor_scalar(msg, msg, 0.0, None, ALU.max).then_inc(msg_ready, 1)

            def aggregate_low(g):
                dve.wait_ge(agg_hi_ready, g + 1)
                nc.vector.tensor_tensor(agg_lo[:], agg_ps[:], agg_hi[:].bitcast(F32), ALU.subtract).then_inc(agg_lo_ready, 1)

            def v_of(g, parity, c):
                if c == 0:
                    dve.wait_ge(rms_done, g + 1)
                dve.wait_ge(hb_ready[c], g + 1)
                need(dve, silu_ready[(c + 2) % HC], g + (1 if c >= 2 else 0))
                nc.vector.tensor_tensor(v[:, c % 2], rms_ps[:], hb[:, parity, c], ALU.mult).then_inc(v_ready[c], 1)

            def masked(g, parity):
                dve.wait_ge(exp_ready, g + 1)
                need_load(dve, mask_loaded, g, parity)
                need(dve, nmp_done, g)
                nc.vector.tensor_tensor(kernel_a, exp_dist, mask_in[:, parity], ALU.mult).then_inc(a_ready, 1)

            def silu_of(g, c):
                dve.wait_ge(tanh_ready[c], g + 1)
                need(dve, silu_lo_ready[(c + 2) % HC], g + (1 if c >= 2 else 0))
                nc.vector.scalar_tensor_tensor(silu[:, c % 2], tanh_v[:, c % 2], 1.0, v[:, c % 2], ALU.add,
                                               ALU.mult).then_inc(silu_ready[c], 1)
                dve.wait_ge(silu_ready[c], g + 1)
                need(dve, w2_done, g)
                nc.vector.tensor_copy(silu_hi[:, c], silu[:, c % 2]).then_inc(silu_hi_ready[c], 1)
                if c == HC - 1:
                    dve.wait_ge(silu_hi_ready[c], g + 1)
                    nc.vector.tensor_tensor(silu_lo[:, c], silu[:, c % 2], silu_hi[:, c].bitcast(F32),
                                            ALU.subtract).then_inc(silu_lo_ready[c], 1)

            def h_minus_n_of(g, parity):
                dve.wait_ge(n_ready, g + 1)
                need(dve, z_part_ready, g)
                nc.vector.tensor_tensor(h_minus_n, h2[:, parity], n_gate, ALU.subtract).then_inc(h_minus_n_ready, 1)

            def z_part_of(g):
                dve.wait_ge(h_minus_n_ready, g + 1)
                dve.wait_ge(tanh_z_ready, g + 1)
                need(dve, out_ready, g)
                nc.vector.scalar_tensor_tensor(z_part, tanh_z, 1.0, h_minus_n, ALU.add, ALU.mult).then_inc(z_part_ready, 1)

            def state(g):
                dve.wait_ge(z_part_ready, g + 1)
                dve.wait_ge(x1_plus_n_ready, g + 1)
                dve.wait_ge(stored, g * 16) if type(g) is not int or g > 0 else None
                nc.vector.scalar_tensor_tensor(out_sb, z_part, 0.5, x1_plus_n, ALU.mult, ALU.add).then_inc(out_ready, 1)

            def layernorm1_stats(g, parity):
                need_load(dve, x_loaded, g, parity)
                for j in range(PER):
                    last = nc.vector.bn_stats(stats1[:, j], x_in[:, parity, j])
                last.then_inc(stats1_ready, 1)

            def layernorm1_moments(g):
                need(dve, rstd1_ready, g)
                dve.wait_ge(stats1_ready, g + 1)
                nc.vector.memset(var1[:], 0.0)
                for j in range(PER):
                    last = nc.vector.bn_aggr(moments1[:, j], stats1[:, j])
                last.then_inc(moments1_ready, 1)
                dve.wait_ge(moments1_ready, g + 1)
                nc.vector.tensor_scalar(var1[:], moments1[:, :, 1], LN_EPS, None, ALU.add).then_inc(var1_ready, 1)

            def layernorm1_shift(g):
                dve.wait_ge(rstd1_ready, g + 1)
                need(dve, h1_ready, g)
                nc.vector.scalar_tensor_tensor(shift1[:], moments1[:, :, 0], -1.0, rstd1[:], ALU.mult, ALU.mult).then_inc(
                    shift1_ready, 1)

            def gathered_low(g):
                dve.wait_ge(nmp_hi_ready, g + 1)
                nc.vector.tensor_tensor(nmp_lo[:], nmp_ps[:], nmp_hi[:].bitcast(F32), ALU.subtract).then_inc(nmp_lo_ready, 1)

            def residual1(g, parity):
                dve.wait_ge(w2_done, g + 1)
                need_load(dve, xT_loaded, g, parity)
                need(dve, x1_plus_n_ready, g - 1)
                nc.vector.scalar_tensor_tensor(x1[:, parity], w2_ps[:], bias("b2"), xT_in[:, parity], ALU.add,
                                               ALU.add).then_inc(x1_ready, 1)

            def square_sum(g):
                dve.wait_ge(sq_pairs, g + 1)
                nc.vector.tensor_tensor(sq[:, 0], sq[:, 0], sq[:, 2], ALU.add).then_inc(sq_sum_ready, 1)

            def mean_square_eps(g):
                dve.wait_ge(sq_nodes_done, g + 1)
                need(dve, rms_ready, g)
                nc.vector.tensor_reduce(sq_total[:], sq_nodes_ps[:].rearrange("p (g f) -> p g f", g=PER),
                                        mybir.AxisListType.X, ALU.add).then_inc(sq_total_ready, 1)
                dve.wait_ge(sq_total_ready, g + 1)
                nc.vector.tensor_scalar(ms_eps[:], sq_total[:], 1.0 / (HC * P), RMS_EPS, ALU.mult,
                                        ALU.add).then_inc(ms_eps_ready, 1)

            def layernorm2_stats(g):
                dve.wait_ge(x1_nodes_done, g + 1)
                for j in range(PER):
                    last = nc.vector.bn_stats(stats2[:, j], x1_nodes_ps[:, graph(j)])
                last.then_inc(stats2_ready, 1)

            def layernorm2_moments(g):
                need(dve, rstd2_ready, g)
                dve.wait_ge(stats2_ready, g + 1)
                nc.vector.memset(var2[:], 0.0)
                for j in range(PER):
                    last = nc.vector.bn_aggr(moments2[:, j], stats2[:, j])
                last.then_inc(moments2_ready, 1)
                dve.wait_ge(moments2_ready, g + 1)
                nc.vector.tensor_scalar(var2[:], moments2[:, :, 1], LN_EPS, None, ALU.add).then_inc(var2_ready, 1)

            def layernorm2_shift(g):
                dve.wait_ge(rstd2_ready, g + 1)
                need(dve, h2_nodes_ready, g)
                nc.vector.scalar_tensor_tensor(shift2[:], moments2[:, :, 0], -1.0, rstd2[:], ALU.mult, ALU.mult).then_inc(
                    shift2_ready, 1)

            def conv2_even_part(g):
                dve.wait_ge(conv2_done, g + 1)
                dve.wait_ge(mix_ready, g + 1)
                need(dve, conv_sum_ready, g)
                nc.vector.scalar_tensor_tensor(even_part[:], conv2_p2, bn_scale[:, 1:2],
                                               mix_even[:].rearrange("p g i -> p (g i)"), ALU.mult,
                                               ALU.add).then_inc(even_part_ready, 1)

            def conv2_relu(g):
                need(dve, xc_ready, g)
                nc.vector.scalar_tensor_tensor(conv_sum[:, 1:T:2], conv2_p0, bn_scale[:, 1:2],
                                               mix_odd[:].rearrange("p g i -> p (g i)"), ALU.mult, ALU.add)
                dve.wait_ge(even_part_ready, g + 1)
                nc.vector.scalar_tensor_tensor(conv_sum[:, 0:T:2], conv2_p0, bn2_minus[:], even_part[:], ALU.mult,
                                               ALU.add).then_inc(conv_sum_ready, 1)
                dve.wait_ge(conv_sum_ready, g + 1)
                need(dve, xc_lo_ready, g)
                nc.vector.tensor_scalar(xc, conv_sum, bn_bias[:, 1:2], 0.0, ALU.add, ALU.max).then_inc(xc_ready, 1)

            def conv2_split(g):
                dve.wait_ge(xc_ready, g + 1)
                need(dve, in_done, g)
                nc.vector.tensor_copy(xc_hi[:], xc).then_inc(xc_hi_ready, 1)
                dve.wait_ge(xc_hi_ready, g + 1)
                nc.vector.tensor_tensor(xc_lo[:], xc, xc_hi[:].bitcast(F32), ALU.subtract).then_inc(xc_lo_ready, 1)

            def h2_low(g, parity):
                dve.wait_ge(h2_ready, g + 1)
                need(dve, hn_done, g)
                nc.vector.tensor_tensor(h2_lo[:], h2[:, parity], h2_hi[:].bitcast(F32), ALU.subtract).then_inc(h2_lo_ready, 1)

            def step(t, parity):
                if peeled(t, 0):
                    dve.wait_ge(b_msg_loaded, 16)
                if has(t, 0):
                    conv1_split(t)
                if has(t, -1):
                    reset_and_input(t - 1)
                if has(t, 0):
                    message_bias(t)
                if has(t, 2):
                    aggregate_low(t + 2)
                if has(t, 0):
                    message_relu(t)
                if has(t, 0):
                    conv1_sum_split(t)
                if has(t, 1):
                    v_of(t + 1, 1 - parity, 0)
                    v_of(t + 1, 1 - parity, 1)
                    silu_of(t + 1, 0)
                    v_of(t + 1, 1 - parity, 2)
                    silu_of(t + 1, 1)
                    v_of(t + 1, 1 - parity, 3)
                    silu_of(t + 1, 2)
                if has(t, 0):
                    masked(t, parity)
                if has(t, 1):
                    silu_of(t + 1, 3)
                if has(t, 3):
                    layernorm1_stats(t + 3, 1 - parity)
                    layernorm1_moments(t + 3)
                if peeled(t, -3):
                    epsilon_identity()
                if has(t, 1):
                    residual1(t + 1, 1 - parity)
                if peeled(t, NG):
                    h_minus_n_of(t - 1, 1 - parity)
                if has(t, -1):
                    z_part_of(t - 1)
                if has(t, 0):
                    gathered_low(t)
                if has(t, -1):
                    state(t - 1)
                if has(t, 3):
                    layernorm1_shift(t + 3)
                if peeled(t, -3):
                    split_low("w1")
                    derived_vectors()
                if peeled(t, -2):
                    split_low("layer1")
                    split_high("conv2")
                if has(t, 1):
                    layernorm2_stats(t + 1)
                    layernorm2_moments(t + 1)
                if has(t, 2) and not peeled(t, -1):
                    square_sum(t + 2)
                if has(t, 0):
                    conv2_even_part(t)
                if has(t, 1):
                    layernorm2_shift(t + 1)
                if peeled(t, -1):
                    split_low("conv2")
                    square_sum(t + 2)
                if has(t, 0):
                    conv2_relu(t)
                if has(t, 0):
                    conv2_split(t)
                if has(t, 2) and not peeled(t, -1):
                    mean_square_eps(t + 2)
                if has(t, 1):
                    h2_low(t + 1, 1 - parity)
                if peeled(t, -1):
                    mean_square_eps(t + 2)

            steps(dve, step)

        @block.gpsimd
        def _(pool):
            nc.gpsimd.memset(eye[:], 0.0).then_inc(eye_zeroed, 1)
            pool.wait_ge(eye_zeroed, 1)
            nc.gpsimd.affine_select(out=eye[:], in_=eye[:], compare_op=ALU.not_equal, fill=1.0, base=0,
                                    pattern=[[-1, P]], channel_multiplier=1).then_inc(eye_ready, 1)
            pool.wait_ge(const_ready, 1)

            def pair_weights():
                pool.wait_ge(raw_ready["conv2"], 16)
                taps = w_raw[:, W_AT["conv2"]:W_AT["conv2"] + 2 * HALF * P].rearrange("p (a two n) -> p a two n", two=2, n=P)
                pairs = w_raw[:, W_AT["conv2_pairs"]:W_TOTAL].rearrange("p (a n) -> p a n", n=P)
                nc.gpsimd.tensor_tensor(pairs, taps[:, :, 0], taps[:, :, 1], ALU.add).then_inc(raw_ready["pairs"], 1)

            def split_low(lot):
                pool.wait_ge(hi_ready[lot], 1)
                nc.gpsimd.tensor_tensor(w_lo[:, lot_cols[lot]], w_raw[:, lot_cols[lot]], w_hi[:, lot_cols[lot]].bitcast(F32),
                                        ALU.subtract).then_inc(lo_ready[lot], 1)

            def h_minus_n_of(g, parity):
                pool.wait_ge(n_ready, g + 1)
                need(pool, z_part_ready, g)
                nc.gpsimd.tensor_tensor(h_minus_n, h2[:, parity], n_gate, ALU.subtract).then_inc(h_minus_n_ready, 1)

            def x1_plus_n_of(g, parity):
                pool.wait_ge(n_ready, g + 1)
                need(pool, out_ready, g)
                nc.gpsimd.tensor_tensor(x1_plus_n, x1[:, parity], n_gate, ALU.add).then_inc(x1_plus_n_ready, 1)

            def conv2_mix(g, parity):
                pool.wait_ge(p1_ready, g + 1)
                need(pool, conv_sum_ready, g)
                h = h2[:, parity].rearrange("p (g i ph) -> p g i ph", g=PER, ph=2)
                nc.gpsimd.tensor_tensor(mix_even[:], h[:, :, :, 0], p1[:, :, 0:PH], ALU.subtract)
                nc.gpsimd.tensor_tensor(mix_odd[:], h[:, :, :, 1], p1[:, :, 1:PH + 1], ALU.add).then_inc(mix_ready, 1)

            def silu_low(g):
                for c in range(HC - 1):
                    pool.wait_ge(silu_hi_ready[c], g + 1)
                    nc.gpsimd.tensor_tensor(silu_lo[:, c], silu[:, c % 2], silu_hi[:, c].bitcast(F32),
                                            ALU.subtract).then_inc(silu_lo_ready[c], 1)

            def square_pairs(g):
                pool.wait_ge(sq_ready[1], g + 1)
                nc.gpsimd.tensor_tensor(sq[:, 0], sq[:, 0], sq[:, 1], ALU.add)
                pool.wait_ge(sq_ready[3], g + 1)
                nc.gpsimd.tensor_tensor(sq[:, 2], sq[:, 2], sq[:, 3], ALU.add).then_inc(sq_pairs, 1)

            def rstd1_of(g):
                pool.wait_ge(var1_ready, g + 1)
                need(pool, h1_ready, g)
                nc.gpsimd.tensor_tensor(rstd1[:], var1[:], minus_half[:], ALU.pow).then_inc(rstd1_ready, 1)

            def adjacency_eps(g, parity):
                need_load(pool, adj_loaded, g, parity)
                need(pool, agg_done, g)
                nc.gpsimd.tensor_tensor(adj_eps[:], adj_in[:, parity], eps_eye[:], ALU.add).then_inc(adj_eps_ready, 1)

            def rms_of(g):
                pool.wait_ge(ms_eps_ready, g + 1)
                need(pool, rms_done, g)
                nc.gpsimd.tensor_tensor(rms[:], ms_eps[:], minus_half[:], ALU.pow).then_inc(rms_ready, 1)

            def rstd2_of(g):
                pool.wait_ge(var2_ready, g + 1)
                need(pool, h2_nodes_ready, g)
                nc.gpsimd.tensor_tensor(rstd2[:], var2[:], minus_half[:], ALU.pow).then_inc(rstd2_ready, 1)

            def step(t, parity):
                if has(t, -1):
                    if not peeled(t, NG):
                        h_minus_n_of(t - 1, 1 - parity)
                    x1_plus_n_of(t - 1, 1 - parity)
                if has(t, 1):
                    silu_low(t + 1)
                if has(t, 0):
                    conv2_mix(t, parity)
                if has(t, 3):
                    rstd1_of(t + 3)
                filling = type(t) is int and t < 0
                if has(t, 3) and filling:
                    if t == -3:
                        pool.wait_ge(eps_eye_ready, 1)
                    adjacency_eps(t + 3, 1 - parity)
                if has(t, 2) and not filling or peeled(t, -2):
                    square_pairs(t + 2)
                if has(t, 1):
                    rstd2_of(t + 1)
                if peeled(t, -1):
                    square_pairs(t + 2)
                if has(t, 2):
                    rms_of(t + 2)
                if has(t, 3) and not filling:
                    adjacency_eps(t + 3, 1 - parity)
                if peeled(t, -2):
                    pair_weights()
                    split_low("ih")
                if peeled(t, -1):
                    split_low("pairs")

            steps(pool, step)


def kernel(x, adj, **p):
    import concourse.bacc as bacc
    from concourse.bass_utils import run_bass_kernel_spmd

    def grouped(a, order):
        a = np.asarray(a).reshape(NG, PER, P, P).transpose(0, *(1 + k for k in order))
        return np.ascontiguousarray(a.reshape(NG, P, T))

    arr = {k: np.asarray(a) for k, a in p.items()}
    g1 = lambda name: arr["L1_gnn_" + name]
    w_se = np.zeros((P, P), np.float32)
    bse = np.zeros(P, np.float32)
    for q in range(3):
        w_se[:, 32 * q:32 * q + SEEDS] = g1("w_se").T
        bse[32 * q:32 * q + SEEDS] = g1("b_se")
    parts = {
        "w1": arr["L0_gnn_W1"],
        "conv1": g1("conv1_w")[:, :, 0].T,
        "se": w_se,
        "hh": g1("w_hh").T,
        "w2": arr["L0_gnn_W2"].reshape(HC, P, P).transpose(1, 0, 2).reshape(P, HC * P),
        "ih": g1("w_ih").reshape(3 * P, 2, P).transpose(2, 1, 0).reshape(P, 6 * P),
        "conv2": g1("conv2_w").transpose(1, 2, 0).reshape(P, TAPS * P),
    }
    weights = np.concatenate([parts[n] for n in W_COLS if n in parts], axis=1)
    vectors = {"b2": arr["L0_gnn_b2"]}
    for name, constant_rows in (("dist_l", slice(64, 96)), ("dist_r", slice(32, 64))):
        vectors[name + "_scale"] = np.ones(P, np.float32)
        vectors[name + "_scale"][constant_rows] = 0
        vectors[name + "_bias"] = bse.copy()
        vectors[name + "_bias"][constant_rows] = -0.5
    for c in range(HC):
        vectors[f"b1_{c}"] = arr["L0_gnn_b1"][c * P:(c + 1) * P]
        vectors[f"rms_{c}"] = arr["L0_gnn_rms_weight"][c * P:(c + 1) * P]
    for n in ("bn1", "bn2"):
        for k in "gbmv":
            vectors[f"{n}_{k}"] = g1(f"{n}_{k}")
    for i, gate in enumerate("rzn"):
        vectors[f"bih_{gate}"] = g1("b_ih")[i * P:(i + 1) * P]
        vectors[f"bhh_{gate}"] = g1("b_hh")[i * P:(i + 1) * P]
    inputs = {
        "x_nodes": grouped(x, (1, 0, 2)),
        "x_feats": grouped(x, (2, 0, 1)),
        "adj_t": grouped(adj, (2, 0, 1)),
        "weights": np.ascontiguousarray(weights),
        "w_msg": np.ascontiguousarray(g1("w_msg").T),
        "vectors": np.ascontiguousarray(np.stack([vectors[n] for n in V_NAMES], axis=1)),
        "b_msg": np.ascontiguousarray(np.tile(g1("b_msg"), PER)),
        "epsilon": arr["L0_gnn_epsilon"].reshape(1),
    }
    nc = bacc.Bacc("TRN2", target_bir_lowering=False, num_devices=1)
    args = [nc.dram_tensor(n, a.shape, mybir.dt.from_np(a.dtype), kind="ExternalInput").ap() for n, a in inputs.items()]
    out = nc.dram_tensor("out", (NG, P, T), F32, kind="ExternalOutput").ap()
    build(nc, *args, out)
    r = run_bass_kernel_spmd(nc, [inputs], core_ids=[0])
    got = r.results[0]["out"]
    return got.reshape(NG, P, PER, P).transpose(0, 2, 3, 1).reshape(GRAPHS, P, P)
```
